# Optimizing a Trainium2 kernel written in Bass

```python
import numpy as np
import jax
import jax.numpy as jnp

def _softmax(x, axis=-1):
    return jax.nn.softmax(x, axis=axis)

def _gelu(x):
    return jax.nn.gelu(x, approximate=True)

def _silu(x):
    return jax.nn.silu(x)

def _sigmoid(x):
    return jax.nn.sigmoid(x)

def _layernorm(x, axis=-1, eps=1e-05):
    m = jnp.mean(x, axis=axis, keepdims=True)
    v = jnp.var(x, axis=axis, keepdims=True)
    return (x - m) / jnp.sqrt(v + eps)

def _scatter_add(tgt, idx, src, axis=0):
    return tgt.at[idx].add(src)

def _segment_sum(src, seg, n):
    return jax.ops.segment_sum(src, seg, n)
kernel_name = 'mk_perceiver_d1_seqx_r4_27042a'

def setup_inputs(seed: int=0):
    np.random.seed(seed)
    _w = jnp.asarray

    def _rec_inputs():
        import jax
        import jax.numpy as jnp
        _rk = jax.random.key(seed)
        x = -0.000125 + 0.9999 * jax.random.normal(jax.random.fold_in(_rk, 1), (16, 64, 512), jnp.float32)
        _lenS = 64 - jax.random.randint(jax.random.fold_in(_rk, 7), (16,), 0, max(1, 64 // 4) + 1, jnp.int32)
        _lenS2 = 256 - jax.random.randint(jax.random.fold_in(_rk, 8), (16,), 0, max(1, 256 // 4) + 1, jnp.int32)
        _ctx_2048P = jax.random.normal(jax.random.fold_in(_rk, 11), (16, 16, 512), jnp.float32)
        _ctx_2048c = jax.random.dirichlet(jax.random.fold_in(_rk, 511), 0.3 * jnp.ones((16,), jnp.float32), (16, 256))
        _ctx_2048t = jnp.einsum('bsk,bkd->bsd', _ctx_2048c, _ctx_2048P)
        _ctx_2048t = _ctx_2048t * jax.lax.rsqrt(jnp.mean(jnp.square(_ctx_2048t)) + 1e-12) * 0.953939
        ctx_2048 = -0.000514642 + 1.00011 * (_ctx_2048t + 0.3 * jax.random.normal(jax.random.fold_in(_rk, 611), (16, 256, 512), jnp.float32))
        _validS = jnp.arange(64)[None, :] < _lenS[:, None]
        _validS2 = jnp.arange(256)[None, :] < _lenS2[:, None]
        _causal = jnp.tril(jnp.ones((64, 64), dtype=bool))
        mask_BxS2_bk0 = jnp.logical_not(jnp.broadcast_to(_validS2[:, :], (16, 256)))
        return (x, ctx_2048, mask_BxS2_bk0)
    x, ctx_2048, mask_BxS2_bk0 = _rec_inputs()

    def _L0_xattn_setup():
        import jax, jax.numpy as jnp
        import numpy as np
        key = jax.random.key(seed)
        k1, k2, k3 = jax.random.split(key, 3)
        B, S, D, M = (8, 512, 512, 128)
        hidden_states = jax.random.normal(k1, (B, S, D), dtype=jnp.float32)
        memory_tokens = jax.random.normal(k2, (B, M, D), dtype=jnp.float32)
        memory_mask = jax.random.randint(k3, (B, M), 0, 2).astype(jnp.bool_)
        return {'hidden_states': hidden_states, 'memory_tokens': memory_tokens, 'memory_mask': memory_mask}
    _L0_xattn_all = _L0_xattn_setup()
    _L0_xattn_in = {k: v for k, v in _L0_xattn_all.items() if k in ()}
    del _L0_xattn_all

    def _L0_attn_setup():
        import jax, jax.numpy as jnp
        import numpy as np
        D_MODEL = 512
        N_HEAD = 16
        HEAD_DIM = D_MODEL // N_HEAD
        SCALE = 1.0 / HEAD_DIM ** 0.5
        key = jax.random.key(seed)
        kx, kq, kk, kv, ko = jax.random.split(key, 5)
        std = 1.0 / np.sqrt(D_MODEL)
        return {'x': jax.random.normal(kx, (2, 512, D_MODEL), dtype=jnp.float32), 'w_q': jax.random.normal(kq, (D_MODEL, D_MODEL), dtype=jnp.float32) * std, 'w_k': jax.random.normal(kk, (D_MODEL, D_MODEL), dtype=jnp.float32) * std, 'w_v': jax.random.normal(kv, (D_MODEL, D_MODEL), dtype=jnp.float32) * std, 'w_o': jax.random.normal(ko, (D_MODEL, D_MODEL), dtype=jnp.float32) * std}
    _L0_attn_all = _L0_attn_setup()
    _L0_attn_in = {k: v for k, v in _L0_attn_all.items() if k in ('w_q', 'w_k', 'w_v', 'w_o')}
    del _L0_attn_all

    def _L0_ffn_setup():
        import jax, jax.numpy as jnp
        import numpy as np
        HIDDEN = 512
        NUM_EXPERTS = 32
        TOP_K = 4
        MOE_INTER = 192
        GROUP = 2
        NUM_CHUNK = NUM_EXPERTS // GROUP
        CHUNK_INTER = 128
        SMALL_SCALE = 0.05

        def _routing(x2d, gate_w):
            logits = x2d @ gate_w.T
            rw = jax.nn.softmax(logits.astype(jnp.float32), axis=-1)
            scores = jax.nn.sigmoid(logits.astype(jnp.float32))
            _, sel = jax.lax.top_k(scores, TOP_K)
            w = jnp.take_along_axis(rw, sel, axis=-1)
            w = w / w.sum(axis=-1, keepdims=True)
            return (w.astype(x2d.dtype), sel)

        def _moe(x2d, Wg, Wu, Wd, cw):
            g = jnp.einsum('th,ehi->eti', x2d, Wg)
            u = jnp.einsum('th,ehi->eti', x2d, Wu)
            a = jax.nn.silu(g) * u * cw.T[:, :, None]
            return jnp.einsum('eti,eih->th', a, Wd)
        key = jax.random.key(seed)
        ks = jax.random.split(key, 8)
        s = 0.02
        B, S = (2, 512)
        return {'hidden_states': jax.random.normal(ks[0], (B, S, HIDDEN), jnp.float32), 'gate_w': jax.random.normal(ks[1], (NUM_EXPERTS, HIDDEN), jnp.float32) * s, 'Wg': jax.random.normal(ks[2], (NUM_EXPERTS, HIDDEN, MOE_INTER), jnp.float32) * s, 'Wu': jax.random.normal(ks[3], (NUM_EXPERTS, HIDDEN, MOE_INTER), jnp.float32) * s, 'Wd': jax.random.normal(ks[4], (NUM_EXPERTS, MOE_INTER, HIDDEN), jnp.float32) * s, 'cWg': jax.random.normal(ks[5], (NUM_CHUNK, HIDDEN, CHUNK_INTER), jnp.float32) * s, 'cWu': jax.random.normal(ks[6], (NUM_CHUNK, HIDDEN, CHUNK_INTER), jnp.float32) * s, 'cWd': jax.random.normal(ks[7], (NUM_CHUNK, CHUNK_INTER, HIDDEN), jnp.float32) * s}
    _L0_ffn_all = _L0_ffn_setup()
    _L0_ffn_in = {k: v for k, v in _L0_ffn_all.items() if k in ('gate_w', 'Wg', 'Wu', 'Wd', 'cWg', 'cWu', 'cWd')}
    del _L0_ffn_all
    return {'x': x, 'ctx_2048': ctx_2048, 'mask_BxS2_bk0': mask_BxS2_bk0, 'L0_attn_w_q': _L0_attn_in['w_q'], 'L0_attn_w_k': _L0_attn_in['w_k'], 'L0_attn_w_v': _L0_attn_in['w_v'], 'L0_attn_w_o': _L0_attn_in['w_o'], 'L0_ffn_gate_w': _L0_ffn_in['gate_w'], 'L0_ffn_Wg': _L0_ffn_in['Wg'], 'L0_ffn_Wu': _L0_ffn_in['Wu'], 'L0_ffn_Wd': _L0_ffn_in['Wd'], 'L0_ffn_cWg': _L0_ffn_in['cWg'], 'L0_ffn_cWu': _L0_ffn_in['cWu'], 'L0_ffn_cWd': _L0_ffn_in['cWd']}

def reference(x, ctx_2048, mask_BxS2_bk0, L0_attn_w_q, L0_attn_w_k, L0_attn_w_v, L0_attn_w_o, L0_ffn_gate_w, L0_ffn_Wg, L0_ffn_Wu, L0_ffn_Wd, L0_ffn_cWg, L0_ffn_cWu, L0_ffn_cWd):
    import jax
    import jax.numpy as jnp

    def _L0_xattn_ref(hidden_states, memory_tokens, memory_mask):
        import jax, jax.numpy as jnp
        import numpy as np
        B, S, D = hidden_states.shape
        scale = 1.0 / jnp.sqrt(jnp.asarray(D, hidden_states.dtype))
        scores = jnp.einsum('bsd,bmd->bsm', hidden_states, memory_tokens) * scale
        neg_inf = jnp.asarray(-1e+30, scores.dtype)
        scores = jnp.where(memory_mask[:, None, :], scores, neg_inf)
        attn = jax.nn.softmax(scores, axis=-1)
        readout = jnp.einsum('bsm,bmd->bsd', attn, memory_tokens)
        valid_b = jnp.any(memory_mask, axis=-1)
        out = jnp.where(valid_b[:, None, None], readout, jnp.zeros_like(readout))
        return out

    def _L0_attn_ref(x, w_q, w_k, w_v, w_o):
        import jax, jax.numpy as jnp
        import numpy as np
        D_MODEL = 512
        N_HEAD = 16
        HEAD_DIM = D_MODEL // N_HEAD
        SCALE = 1.0 / HEAD_DIM ** 0.5
        b, s, d = x.shape

        def proj(w):
            y = jnp.einsum('bsd,ed->bse', x, w)
            return y.reshape(b, s, N_HEAD, HEAD_DIM).transpose(0, 2, 1, 3)
        q, k, v = (proj(w_q), proj(w_k), proj(w_v))
        scores = jnp.einsum('bhqd,bhkd->bhqk', q, k) * SCALE
        probs = jax.nn.softmax(scores, axis=-1)
        attn = jnp.einsum('bhqk,bhkd->bhqd', probs, v)
        attn = attn.transpose(0, 2, 1, 3).reshape(b, s, d)
        return jnp.einsum('bsd,ed->bse', attn, w_o)

    def _L0_ffn_ref(hidden_states, gate_w, Wg, Wu, Wd, cWg, cWu, cWd):
        import jax, jax.numpy as jnp
        import numpy as np
        HIDDEN = 512
        NUM_EXPERTS = 32
        TOP_K = 4
        MOE_INTER = 192
        GROUP = 2
        NUM_CHUNK = NUM_EXPERTS // GROUP
        CHUNK_INTER = 128
        SMALL_SCALE = 0.05

        def _routing(x2d, gate_w):
            logits = x2d @ gate_w.T
            rw = jax.nn.softmax(logits.astype(jnp.float32), axis=-1)
            scores = jax.nn.sigmoid(logits.astype(jnp.float32))
            _, sel = jax.lax.top_k(scores, TOP_K)
            w = jnp.take_along_axis(rw, sel, axis=-1)
            w = w / w.sum(axis=-1, keepdims=True)
            return (w.astype(x2d.dtype), sel)

        def _moe(x2d, Wg, Wu, Wd, cw):
            g = jnp.einsum('th,ehi->eti', x2d, Wg)
            u = jnp.einsum('th,ehi->eti', x2d, Wu)
            a = jax.nn.silu(g) * u * cw.T[:, :, None]
            return jnp.einsum('eti,eih->th', a, Wd)
        B, S, H = hidden_states.shape
        T = B * S
        x = hidden_states.reshape(T, H)
        w, sel = _routing(x, gate_w)
        rows = jnp.arange(T)[:, None]
        cw_large = jnp.zeros((T, NUM_EXPERTS), x.dtype).at[rows, sel].add(w)
        cw_small = jnp.zeros((T, NUM_CHUNK), x.dtype).at[rows, sel // GROUP].add(w)
        large = _moe(x, Wg, Wu, Wd, cw_large)
        small = _moe(x, cWg, cWu, cWd, cw_small)
        return (large + SMALL_SCALE * small).reshape(B, S, H)
    x = x + _L0_xattn_ref(_layernorm(x, axis=-1), ctx_2048, mask_BxS2_bk0)
    x = x + _L0_attn_ref(_layernorm(x, axis=-1), L0_attn_w_q, L0_attn_w_k, L0_attn_w_v, L0_attn_w_o)
    x = x + _L0_ffn_ref(_layernorm(x, axis=-1), L0_ffn_gate_w, L0_ffn_Wg, L0_ffn_Wu, L0_ffn_Wd, L0_ffn_cWg, L0_ffn_cWu, L0_ffn_cWd)
    return x

_drawn_inputs = setup_inputs


def setup_inputs(seed=0):
    import zlib

    import numpy as np

    out = dict(_drawn_inputs(seed))
    spreads = {}
    factors = {'L0_ffn_gate_w': 4.938,
     'L0_ffn_Wg': 4.668,
     'L0_ffn_Wu': 4.523,
     'L0_ffn_Wd': 4.534,
     'L0_ffn_cWg': 8.0,
     'L0_ffn_cWu': 8.0,
     'L0_ffn_cWd': 8.0}
    for name, (base, spread) in spreads.items():
        noise = np.random.default_rng([zlib.crc32(name.encode()), seed]).standard_normal(out[name].shape)
        drawn = base * np.exp(spread * noise) if base else spread * noise
        out[name] = jnp.asarray(drawn.astype(out[name].dtype))
    for name, factor in factors.items():
        out[name] = (out[name] * factor).astype(out[name].dtype)
    return out
```

```python
from contextlib import ExitStack

import concourse.bass as bass
from concourse import mybir

F32 = mybir.dt.float32
F32R = mybir.dt.float32r
BF16 = mybir.dt.bfloat16
I32 = mybir.dt.int32
U32 = mybir.dt.uint32
U8 = mybir.dt.uint8
ALU = mybir.AluOpType
ACT = mybir.ActivationFunctionType
AX = mybir.AxisListType

P = 128
CREDIT = 2
DMA = 16
CAP = 208
EPS = 1e-5
NEG = 1e30
SMALL_SCALE = 0.05
LINKS = 30


def most_blocks(experts, tokens, choices):
    best = {0: 0}
    for _ in range(experts):
        new = dict(best)
        for blocks, used in best.items():
            for m in range(1, -(-(tokens - CAP) // P) + 1):
                cost = used + CAP + (m - 1) * P + 1
                if cost <= choices and cost < new.get(blocks + m, choices + 1):
                    new[blocks + m] = cost
        best = new
    return max(best)


def perceiver_moe(nc, x, ctx_in, mask, w_q, w_k, w_v, w_o, gate_w, Wg, Wu, Wd, cWg, cWu, cWd, out):
    B, S, D = x.shape
    M = ctx_in.shape[1]
    E, _, FI = Wg.shape
    CI = cWg.shape[2]
    NC = D // P
    T = B * S // P
    BT = P // S
    HD = 32
    H = D // HD
    MC = BT * M // P
    TOPK = 4
    F2 = FI - P
    OVB = -(-(B * S - CAP) // P)
    REGION = CAP + OVB * P
    LISTW = -(-E * REGION // P)
    KMAX = most_blocks(E, B * S, TOPK * B * S)
    YROWS = E * CAP + KMAX * P
    CAP2 = CAP - P
    XS_SCALE = float(D) ** -0.5
    SS_SCALE = float(HD) ** -0.5
    assert BT == 2 and T % 2 == 0 and H * S == 1024 and E * REGION == LISTW * P and CI == P and F2 == 64

    mask = mask.bitcast(U8)
    xf = x.rearrange("b s d -> (b s) d")
    cf = ctx_in.rearrange("b m d -> (b m) d")
    of = out.rearrange("b s d -> (b s) d")

    xn_dram = nc.dram_tensor("xn_scratch", (B * S, D), F32, kind="Internal").ap()
    x2_dram = nc.dram_tensor("x2_scratch", (B * S, D), F32, kind="Internal").ap()
    list_dram = nc.dram_tensor("list_scratch", (E * REGION, 1), I32, kind="Internal").ap()
    y_dram = nc.dram_tensor("y_scratch", (YROWS, D), F32, kind="Internal").ap()

    with ExitStack() as stack:
        def sb(name, shape, dt=F32):
            return stack.enter_context(nc.sbuf_tensor(name, shape, dt))

        def sem(name):
            return stack.enter_context(nc.semaphore(name))

        tpair = stack.enter_context(nc.psum_tensor("tpair", [P, 2, 512], F32))
        bank2 = stack.enter_context(nc.psum_tensor("bank2", [P, 512], F32))
        pair = stack.enter_context(nc.psum_tensor("pair", [P, 2, 512], F32))
        bank5 = stack.enter_context(nc.psum_tensor("bank5", [P, 512], F32))
        bank6 = stack.enter_context(nc.psum_tensor("bank6", [P, 512], F32))
        bank7 = stack.enter_context(nc.psum_tensor("bank7", [P, 512], F32))
        tp = [tpair[:, 0, :], tpair[:, 1, :]]
        xb = bank2
        s2 = pair
        qo = bank5
        ko = bank6
        vl = bank7

        ident = sb("ident", [P, P])
        tri = sb("tri", [P, P], BF16)
        ones = sb("ones", [P, P], BF16)
        neghalf = sb("neghalf", [P, 1])
        iota_e = sb("iota_e", [P, E])
        base_e = sb("base_e", [P, E])
        zlist = sb("zlist", [P, LISTW], I32)

        wT = {n: sb(f"{n}T", [P, NC, D]) for n in ("wq", "wk", "wv", "wo")}
        gateT = sb("gateT", [P, NC, E])
        x_in = sb("x_in", [P, 2, D])
        ctx_sb = sb("ctx_sb", [P, 2, MC, D])
        mask_u8 = sb("mask_u8", [P, 2, M], U8)
        maskb = sb("maskb", [P, M])
        valid = sb("valid", [P, 1])
        ctxT_buf = sb("ctxT_buf", [P, NC * MC * P])
        ctxT = ctxT_buf[:, :].rearrange("p (c n) -> p c n", c=NC)
        stat = sb("stat", [P, 3, 6])
        mv = sb("mv", [P, 3, 2])
        vare = sb("vare", [P, 3])
        rstd = sb("rstd", [P, 3])
        xn1 = sb("xn1", [P, D])
        xn2 = sb("xn2", [P, D])
        xn3 = sb("xn3", [P, 2, D])
        xn1T = sb("xn1T", [P, NC, P])
        xn2T = sb("xn2T", [P, NC, P])
        xn3T = sb("xn3T", [P, NC, P])
        xsc = sb("xsc", [P, M])
        xmax = sb("xmax", [P, 1])
        xnb = sb("xnb", [P, 1])
        xsum = sb("xsum", [P, 1])
        xrs = sb("xrs", [P, 1])
        xrv = sb("xrv", [P, 1])
        xp = sb("xp", [P, BT * M])
        xpT = sb("xpT", [P, MC, P])
        x1 = sb("x1", [P, D])
        x2 = sb("x2", [P, 2, D])
        qT = sb("qT", [P, NC, P])
        kT = sb("kT", [P, NC, P])
        v_sb = sb("v_sb", [P, D])
        v_swap = sb("v_swap", [P, D])
        smax = sb("smax", [P, H])
        ssum = sb("ssum", [P, H])
        srec = sb("srec", [P, H])
        probs_buf = sb("probs_buf", [P, 2 * H * S])
        sp_sb = probs_buf[:, 0:H * S].rearrange("p (h k) -> p h k", k=S)
        pT = probs_buf[:, H * S:].rearrange("p (j q) -> p j q", q=P)
        attnT = sb("attnT", [P, NC, P])
        logit = sb("logit", [P, E])
        lmax = sb("lmax", [P, 1])
        enl = sb("enl", [P, E])
        el = sb("el", [P, E])
        sg1 = sb("sg1", [P, E])
        score = sb("score", [P, E])
        top8 = sb("top8", [P, 8])
        idx8 = sb("idx8", [P, 8], U32)
        idxf = sb("idxf", [P, TOPK])
        hot = sb("hot", [P, TOPK, E])
        sel = sb("sel", [P, E], BF16)
        prod = sb("prod", [P, TOPK, E])
        prod2 = sb("prod2", [P, TOPK, E])
        wraw = sb("wraw", [P, TOPK])
        wn = sb("wn", [P, TOPK])
        wsum = sb("wsum", [P, 1])
        wrec = sb("wrec", [P, 1])
        w_all = sb("w_all", [P, T * TOPK])
        e_all = sb("e_all", [P, T * TOPK])
        s_all = sb("s_all", [P, T * TOPK])
        yrow = sb("yrow", [P, T * TOPK], I32)
        zrow = sb("zrow", [P, D])
        run = sb("run", [P, E])
        slotb = sb("slotb", [P, E])
        slotf = sb("slotf", [P, TOPK])
        slot = sb("slot", [P, 2, TOPK], I32)
        tokf = sb("tokf", [P, 1])
        tok = sb("tok", [P, 2, 1], I32)
        names = ("ln1_var ln1_rstd ln1_done xs_done xmax_done xexp_done xrv_done pv_done x1_done "
                 "ln2_var ln2_rstd ln2_done qk_done v_done qT_done kT_done vsb_done ss_done ssub_done "
                 "sexp_done sp_done av_done attnT_done o_done x2_done ln3_var ln3_rstd ln3_done "
                 "logit_done lmax_done lexp_done sel_done rank_done slot_done").split()
        sig = {n: sem(n) for n in names}
        tp_full = [sem("tp_full0"), sem("tp_full1")]
        tp_copied = [sem("tp_copied0"), sem("tp_copied1")]
        const_ready = sem("const_ready")
        dve_const = sem("dve_const")
        w_loaded = {n: sem(f"{n}_loaded") for n in ("wq", "wk", "wv", "wo", "gate")}
        x_loaded = [sem("x_loaded0"), sem("x_loaded1")]
        swap_done = sem("swap_done")
        x2_stored = [sem("x2_stored0"), sem("x2_stored1")]
        xn_stored = [sem("xn_stored0"), sem("xn_stored1")]
        y_zeroed = sem("y_zeroed")
        list_zeroed = sem("list_zeroed")
        scattered = sem("scattered")
        slots_used = sem("slots_used")
        dve_chain = sem("dve_chain")
        pool_chain = sem("pool_chain")
        settled = sem("settled")
        row_tile_done = sem("row_tile_done")
        lists_ready = sem("lists_ready")

        stage_w = [t[:, :].rearrange("p (c d) -> p c d", d=D) for t in (ctxT_buf, probs_buf)]
        stage_g = sb("stage_g", [E, D])
        meta = sb("meta", [P, E])

        def flat(t):
            return t[:, :, :].rearrange("p a b -> p (a b)")

        raw_gu = [flat(wT[n])[:, 0:2 * NC * FI].rearrange("p (c i) -> p c i", c=NC) for n in ("wq", "wk")]
        raw_d = [flat(wT["wv"])[:, n * 2 * D:(n + 1) * 2 * D].rearrange("p (k d) -> p k d", k=2) for n in range(2)]
        raw_c = flat(wT["wo"])[:, 0:2 * NC * CI].rearrange("p (s c i) -> p s c i", s=2, c=NC)
        raw_cd = flat(wT["wo"])[:, 2 * NC * CI:2 * NC * CI + D]
        gu = [[sb(f"gu_{part}{n}", [P, NC, 2 * FI], F32R) for part in ("hi", "lo")] for n in range(2)]
        dn = [[sb(f"dn_{part}{n}", [P, 2, D], F32R) for part in ("hi", "lo")] for n in range(2)]
        cgu = [[sb(f"cgu_{part}{n}", [P, 2, NC, CI], F32R) for part in ("hi", "lo")] for n in range(2)]
        cdn = [[sb(f"cdn_{part}{n}", [P, D], F32R) for part in ("hi", "lo")] for n in range(2)]
        xT = [[sb(f"xT_{part}{n}", [P, NC, CAP], F32R) for part in ("hi", "lo")] for n in range(2)]
        aT = [[sb(f"aT_{part}{n}", [P, 3, CAP], F32R) for part in ("hi", "lo")] for n in range(2)]
        xg = [ctx_sb[:, n, 0:2, :] for n in range(2)]
        y_sb = [ctx_sb[:, n, 2:4, :] for n in range(2)]
        act_g = sp_sb[:, :, :].rearrange("p h k -> p (h k)")[:, 0:3 * CAP].rearrange("p (k n) -> p k n", k=3)
        act_a = probs_buf[:, H * S:H * S + 3 * CAP].rearrange("p (k n) -> p k n", k=3)
        idx = [sb(f"idx{n}", [P, 2], I32) for n in range(2)]
        g_bank = [xb, pair[:, 0, :], pair[:, 1, :]]
        y_bank = [qo, ko]
        names_b = ("xT_full xhi_done xlo_done whi_done wlo_done gu_done silu_done mul_done dhi_done dlo_done ahi_done "
                   "alo_done y0_full y1_full y0_done y1_done").split()
        sg = {n: sem(n) for n in names_b}
        gu_loaded = [sem("gu_loaded0"), sem("gu_loaded1")]
        d_loaded = [sem("d_loaded0"), sem("d_loaded1")]
        c_loaded = sem("c_loaded")
        cd_loaded = sem("cd_loaded")
        idx_loaded = [sem("idx_loaded0"), sem("idx_loaded1")]
        gathered = [sem("gathered0"), sem("gathered1")]
        y_stored = [sem("y_stored0"), sem("y_stored1")]
        pads_zero = sem("pads_zero")

        meta_f = sb("meta_f", [1, 4, KMAX])
        meta_i = sb("meta_i", [1, 4, KMAX], I32)
        meta_half = sb("meta_half", [1, KMAX], I32)
        sc = ctxT_buf[:, 0:E * E].rearrange("p (a b) -> p a b", b=E)
        sc2 = ctxT_buf[:, E * E:2 * E * E].rearrange("p (a b) -> p a b", b=E)
        cnt = sb("cnt", [P, E])
        nblk = sb("nblk", [P, E])
        cum = sb("cum", [P, E])
        before = sb("before", [P, E])
        over = sb("over", [P, T * TOPK])
        rank = sb("rank", [P, T * TOPK])
        past = sb("past", [P, T * TOPK])
        yrow_ready = sem("yrow_ready")
        ordi = sb("ordi", [1, KMAX])
        lower = sb("lower", [P, E, E], BF16)
        thr = sb("thr", [P, OVB])
        idx_c = sb("idx_c", [P, 1], I32)
        meta_ready = sem("meta_ready")
        sc_names = "c_idx_loaded c_w_loaded c_gathered c_xT_full c_xT_done c_gu_done c_silu_done c_mul_done c_y_full c_y_done c_stored".split()
        sv = {n: sem(n) for n in sc_names}

        y4 = [ctx_sb[:, n, :, :] for n in range(2)]
        slot_d = [sb(f"slot_d{n}", [P, TOPK], I32) for n in range(2)]
        w_d = [sb(f"w_d{n}", [P, TOPK]) for n in range(2)]
        y_complete = sem("y_complete")
        slot_here = sem("slot_here")
        d_loaded_t = [sem("d_loaded_t0"), sem("d_loaded_t1")]
        y4_gathered = [sem("y4_gathered0"), sem("y4_gathered1")]
        sum_done = sem("sum_done")
        out_stored = [sem("out_stored0"), sem("out_stored1")]

        WFILLS = 18
        XFILLS = {"ctx0": 0, "ctx1": 1, "ctx2": 2, "ctx3": 3, "xn1T": 4, "xpT": 5}
        BASE = WFILLS + len(XFILLS)
        LOOP = {"xn2T": 0, "ctx0": 1, "ctx1": 2, "ctx2": 3, "ctx3": 4, "xn1T": 5, "pT0": 6, "pT1": 7, "xpT": 8,
                "xn3T": 9}
        LAST = {"xn2T": 0, "pT0": 1, "pT1": 2, "xn3T": 3}

        def fill_of(t, name, mode):
            if mode == "first":
                k, halves = WFILLS + XFILLS[name], 0
            else:
                k = BASE + (LAST if mode == "last" else LOOP)[name]
                halves = t * (len(LOOP) // 2)
            return k % 2, halves + k // 2

        def wait_copied(eng, t, name, mode):
            b, m = fill_of(t, name, mode)
            eng.wait_ge(tp_copied[b], m + 1)

        block = stack.enter_context(nc.Block())

        def tiles(eng, body):
            with eng.Fori(0, T // 2 - 1) as i:
                body(i * 2, 0, "loop")
                body(i * 2 + 1, 1, "loop")
            body(T - 2, 0, "loop")
            body(T - 1, 1, "last")

        class Expert:

            def __init__(self, i, m):
                self.i, self.m = i, m
                self.e = i * 4 + m
                self.par, self.pair_par = m % 2, m // 2 % 2
                self.half = i * 2 + m // 2
                self.first_of_pair = m % 2 == 0

            def ahead(self, k):
                other = Expert(self.i, self.m + k)
                return None if isinstance(other.e, int) and not 0 <= other.e < E else other

        def experts(eng, step):
            step(Expert(0, 0))
            with eng.Fori(0, E // 4 - 1) as i:
                for m in range(1, 5):
                    step(Expert(i, m))
            for m in range(1, 4):
                step(Expert(E // 4 - 1, m))

        def overflow(eng, step):
            eng.wait_ge(meta_ready, 1)
            count = eng.value_load(meta_i[0:1, 0, 0:1], min_val=0, max_val=KMAX)
            with eng.If(count > 0):
                with eng.Fori(0, count) as k:
                    step(k)

        def outputs(eng, step):
            with eng.Fori(0, T // 2) as i:
                for par in range(2):
                    step(i, par)

        def settle(eng):
            eng.sem_inc(settled, 1)

        def place(h):
            return (h % 2) * 8 + (h % 4) // 2 * 4 + h // 4

        def spread(ap, dim, n):
            shape = list(ap.shape)
            return ap.unsqueeze(dim).broadcast_to(shape[:dim] + [n] + shape[dim:])

        def chunks(ap, n):
            return ap.rearrange("p (c n) -> p c n", n=n)

        @block.sync
        def _(sp):
            for q in (swap_done, x2_stored[0], x2_stored[1], xn_stored[0], xn_stored[1]):
                sp.sem_inc(q, CREDIT * DMA)

            def load_tile(t, par):
                sp.dma_start(x_in[:, par, :], xf[bass.ds(t * P, P), :]).then_inc(x_loaded[par], DMA)
                sp.dma_start(ctx_sb[:, par, :, :], cf[bass.ds(t * (MC * P), MC * P), :].rearrange(
                    "(c p) d -> p c d", p=P)).then_inc(x_loaded[par], DMA)
                for b in range(BT):
                    sp.dma_start(mask_u8[b * S:(b + 1) * S, par, :],
                                 mask[bass.ds(t * BT + b, 1), :].broadcast_to([S, M])).then_inc(x_loaded[par], DMA)

            for n, (name, w) in enumerate((("wq", w_q), ("wk", w_k))):
                sp.dma_start(stage_w[n], w.rearrange("(c p) d -> p c d", p=P)).then_inc(w_loaded[name], DMA)
            sp.dma_start(stage_g[:, :], gate_w).then_inc(w_loaded["gate"], DMA)
            load_tile(0, 0)
            load_tile(1, 1)
            for n, (name, w) in enumerate((("wv", w_v), ("wo", w_o))):
                sp.wait_ge(tp_full[1], 2 * (n + 1))
                sp.dma_start(stage_w[n], w.rearrange("(c p) d -> p c d", p=P)).then_inc(w_loaded[name], DMA)
            sp.wait_ge(const_ready, 1)
            sp.dma_start(list_dram.rearrange("(p n) o -> p (n o)", p=P), zlist[:, :]).then_inc(list_zeroed, DMA)
            sp.dma_start(y_dram[E * CAP:YROWS, :].rearrange("(k p) d -> p k d", p=P),
                         spread(zrow[:, :], 1, KMAX)).then_inc(y_zeroed, DMA)

            def body(t, par, mode):
                sp.wait_ge(sig["vsb_done"], t + 1 + CREDIT)
                sp.wait_ge(sig["av_done"], t + CREDIT)
                sp.dma_start(v_swap[0:S, :], v_sb[S:P, :]).then_inc(swap_done, DMA)
                sp.dma_start(v_swap[S:P, :], v_sb[0:S, :]).then_inc(swap_done, DMA)
                sp.wait_ge(sig["x2_done"], t + 1 + CREDIT)
                sp.dma_start(x2_dram[bass.ds(t * P, P), :], x2[:, par, :]).then_inc(x2_stored[par], DMA)
                sp.wait_ge(sig["ln3_done"], t + 1 + CREDIT)
                sp.dma_start(xn_dram[bass.ds(t * P, P), :], xn3[:, par, :]).then_inc(xn_stored[par], DMA)

            def with_loads(t, par, mode):
                if not (isinstance(t, int) and t + 2 >= T):
                    sp.wait_ge(sig["x1_done"], t + 1 + CREDIT)
                    load_tile(t + 2, par)
                body(t, par, mode)

            tiles(sp, with_loads)
            for q in x2_stored + xn_stored:
                sp.wait_ge(q, CREDIT * DMA + T // 2 * DMA)
            sp.wait_ge(y_zeroed, DMA)

            for q in y_stored:
                sp.sem_inc(q, 2 * CREDIT * DMA)

            def load_gu(x, dst, q):
                for s, w in ((0, Wg), (1, Wu)):
                    sp.dma_start(dst[:, :, s * FI:(s + 1) * FI], w[bass.ds(x, 1)].rearrange("o (p c) i -> (o p) c i", c=NC)).then_inc(q, DMA)

            def load_d(x, dst, q):
                w = Wd[bass.ds(x, 1)].rearrange("o i d -> (o i) d")
                sp.dma_start(dst[:, 0, :], w[FI - P:FI, :]).then_inc(q, DMA)
                sp.dma_start(dst[P - F2:P, 1, :], w[0:F2, :]).then_inc(q, DMA)

            def load_c(x, q):
                for s, w in ((0, cWg), (1, cWu)):
                    sp.dma_start(raw_c[:, s, :, :], w[bass.ds(x, 1)].rearrange("o (p c) i -> (o p) c i", c=NC)).then_inc(q, DMA)

            def load_cd(x, q):
                sp.dma_start(raw_cd, cWd[bass.ds(x, 1)].rearrange("o i d -> (o i) d")).then_inc(q, DMA)

            def load_idx(x):
                sp.dma_start(idx[x.par][:, :], list_dram[bass.ds(x.e * REGION, 2 * P), :].rearrange(
                    "(j p) o -> p (j o)", p=P), allow_slow_non_contiguous=True).then_inc(idx_loaded[x.par], DMA)

            sp.wait_ge(sig["o_done"], T + CREDIT)
            first, second = Expert(0, 0), Expert(0, 1)
            load_gu(0, raw_gu[0], gu_loaded[0])
            load_c(0, c_loaded)
            sp.wait_ge(pads_zero, 1)
            load_d(0, raw_d[0], d_loaded[0])
            load_cd(0, cd_loaded)
            load_gu(1, raw_gu[1], gu_loaded[1])
            sp.wait_ge(lists_ready, 1)
            load_idx(first)
            load_idx(second)

            def store_y(x):
                rows = y_dram[bass.ds(x.e * CAP, CAP), :]
                sp.wait_ge(sg["y0_done"], x.e + 1 + CREDIT)
                sp.dma_start(rows[0:P, :], y_sb[x.par][:, 0, :]).then_inc(y_stored[x.par], DMA)
                sp.wait_ge(sg["y1_done"], x.e + 1 + CREDIT)
                sp.dma_start(rows[P:CAP, :], y_sb[x.par][P - CAP2:P, 1, :]).then_inc(y_stored[x.par], DMA)

            def step(x):
                nxt, nxt2, last = x.ahead(1), x.ahead(2), x.ahead(-1)
                if nxt2 is not None:
                    sp.wait_ge(sg["wlo_done"], x.e + 1 + CREDIT)
                    load_gu(nxt2.e, raw_gu[x.par], gu_loaded[x.par])
                    if x.first_of_pair:
                        load_c(nxt2.half, c_loaded)
                if nxt is not None:
                    if last is not None:
                        sp.wait_ge(sg["dlo_done"], x.e + CREDIT)
                    load_d(nxt.e, raw_d[nxt.par], d_loaded[nxt.par])
                    if nxt.first_of_pair:
                        load_cd(nxt.half, cd_loaded)
                if nxt2 is not None:
                    sp.wait_ge(sg["xT_full"], x.e + 1 + CREDIT)
                    load_idx(nxt2)
                if last is not None:
                    store_y(last)

            experts(sp, step)
            store_y(Expert(E // 4 - 1, 3))
            for q in y_stored:
                sp.wait_ge(q, 2 * CREDIT * DMA + E // 2 * 2 * DMA)

            def block_c(k):
                ek = sp.value_load(meta_i[0:1, 1, bass.ds(k, 1)], min_val=0, max_val=E - 1)
                ck = sp.value_load(meta_i[0:1, 2, bass.ds(k, 1)], min_val=0, max_val=E // 2 - 1)
                rk = sp.value_load(meta_i[0:1, 3, bass.ds(k, 1)], min_val=0, max_val=E * REGION - P)
                sp.dma_start(idx_c[:, :], list_dram[bass.ds(rk, P), :]).then_inc(sv["c_idx_loaded"], DMA)
                load_gu(ek, raw_gu[0], sv["c_w_loaded"])
                load_d(ek, raw_d[0], sv["c_w_loaded"])
                load_c(ck, sv["c_w_loaded"])
                load_cd(ck, sv["c_w_loaded"])
                sp.wait_ge(sv["c_y_done"], k + 1)
                sp.dma_start(y_dram[bass.ds(k * P + E * CAP, P), :], y_sb[0][:, 0, :]).then_inc(sv["c_stored"], DMA)
                sp.wait_ge(sv["c_stored"], (k + 1) * DMA)
                settle(sp)

            overflow(sp, block_c)
            sp.sem_inc(y_complete, 1)

            for q in out_stored:
                sp.sem_inc(q, CREDIT * DMA)

            def tile_d(half, par):
                t = half * 2 + par
                rows = bass.ds(t * P, P)
                sp.wait_ge(sum_done, t - 1 + CREDIT)
                sp.dma_start(x_in[:, par, :], x2_dram[rows, :]).then_inc(d_loaded_t[par], DMA)

            def store_out(t, par):
                sp.wait_ge(sum_done, t + 1 + CREDIT)
                sp.dma_start(of[bass.ds(t * P, P), :], x2[:, par, :]).then_inc(out_stored[par], DMA)

            with sp.Fori(0, T // 2) as i:
                for par in range(2):
                    tile_d(i, par)
                for par in range(2):
                    store_out(i * 2 + par, par)
            for q in out_stored:
                sp.wait_ge(q, CREDIT * DMA + T // 2 * DMA)

        @block.gpsimd
        def _(pool):
            for n in ("ln1_rstd", "ln2_rstd", "ln3_rstd"):
                pool.sem_inc(sig[n], CREDIT)
            pool.sem_inc(slots_used, CREDIT)
            nc.gpsimd.memset(zrow[:, :], 0.0).then_inc(pool_chain, 1)
            nc.gpsimd.memset(zlist[:, :], 0).then_inc(pool_chain, 1)
            nc.gpsimd.memset(ident[:, :], 0.0).then_inc(pool_chain, 1)
            nc.gpsimd.memset(tri[:, :], 0.0).then_inc(pool_chain, 1)
            nc.gpsimd.memset(ones[:, :], 1.0).then_inc(pool_chain, 1)
            nc.gpsimd.memset(neghalf[:, :], -0.5).then_inc(pool_chain, 1)
            nc.gpsimd.iota(iota_e[:, :], [[1, E]], base=0, channel_multiplier=0,
                           allow_small_or_imprecise_dtypes=True).then_inc(pool_chain, 1)
            nc.gpsimd.iota(base_e[:, :], [[REGION, E]], base=0, channel_multiplier=0,
                           allow_small_or_imprecise_dtypes=True).then_inc(pool_chain, 1)
            nc.gpsimd.iota(tokf[:, :], [[0, 1]], base=0, channel_multiplier=1,
                           allow_small_or_imprecise_dtypes=True).then_inc(pool_chain, 1)
            nc.gpsimd.iota(ordi[:, :], [[1, KMAX]], base=0, channel_multiplier=0,
                           allow_small_or_imprecise_dtypes=True).then_inc(pool_chain, 1)
            nc.gpsimd.iota(thr[:, :], [[P, OVB]], base=CAP, channel_multiplier=0,
                           allow_small_or_imprecise_dtypes=True).then_inc(pool_chain, 1)
            nc.gpsimd.memset(lower[:, :, :], 1.0).then_inc(pool_chain, 1)
            pool.wait_ge(pool_chain, 12)
            nc.gpsimd.affine_select(out=lower[:, :, :], in_=lower[:, :, :], compare_op=ALU.is_ge, fill=0.0, base=0,
                                    pattern=[[1, E], [-1, E]], channel_multiplier=0).then_inc(pool_chain, 1)
            nc.gpsimd.affine_select(out=ident[:, :], in_=ident[:, :], compare_op=ALU.not_equal, fill=1.0, base=0,
                                    pattern=[[-1, P]], channel_multiplier=1).then_inc(pool_chain, 1)
            nc.gpsimd.affine_select(out=tri[:, :], in_=tri[:, :], compare_op=ALU.is_ge, fill=1.0, base=0,
                                    pattern=[[-1, P]], channel_multiplier=1).then_inc(pool_chain, 1)
            pool.wait_ge(pool_chain, 15)
            pool.sem_inc(const_ready, 1)

            def power(n, col, t):
                pool.wait_ge(sig[f"{n}_var"], t + 1 + CREDIT)
                nc.gpsimd.tensor_tensor(rstd[:, col:col + 1], vare[:, col:col + 1], neghalf[:, :],
                                        ALU.pow).then_inc(sig[f"{n}_rstd"], 1)

            power("ln1", 0, 0)
            power("ln2", 1, 0)
            pool.wait_ge(list_zeroed, DMA)

            def body(t, par, mode):
                if mode != "last":
                    power("ln1", 0, t + 1)
                power("ln3", 2, t)
                if mode != "last":
                    power("ln2", 1, t + 1)
                pool.wait_ge(sig["slot_done"], t + 1 + CREDIT)
                settle(pool)
                for k in range(TOPK):
                    nc.gpsimd.indirect_dma_start(
                        list_dram, bass.IndirectOffsetOnAxis(ap=slot[:, par, k:k + 1], axis=0),
                        tok[:, par, :], None).then_inc(scattered, DMA)
                pool.wait_ge(scattered, (t + 1) * (TOPK * DMA))
                pool.sem_inc(slots_used, 1)

            tiles(pool, body)
            pool.sem_inc(lists_ready, 1)

            for q in xn_stored:
                pool.wait_ge(q, CREDIT * DMA + T // 2 * DMA)

            def gather(dst, at):
                return nc.gpsimd.indirect_dma_start(dst, None, xn_dram, bass.IndirectOffsetOnAxis(ap=at, axis=0))

            def gather_rows(x):
                pool.wait_ge(idx_loaded[x.par], (x.half + 1) * DMA)
                if not isinstance(x.e, int) or x.e >= 2:
                    pool.wait_ge(sg["xT_full"], x.e - 1 + CREDIT)
                settle(pool)
                gather(xg[x.par][:, 0, :], idx[x.par][:, 0:1]).then_inc(gathered[x.par], DMA)
                gather(xg[x.par][0:CAP2, 1, :], idx[x.par][0:CAP2, 1:2]).then_inc(gathered[x.par], DMA)

            gather_rows(Expert(0, 0))
            gather_rows(Expert(0, 1))

            def step(x):
                if x.ahead(2) is not None:
                    gather_rows(x.ahead(2))

            experts(pool, step)

            def block_c(k):
                pool.wait_ge(sv["c_idx_loaded"], (k + 1) * DMA)
                settle(pool)
                gather(xg[0][:, 0, :], idx_c[:, 0:1]).then_inc(sv["c_gathered"], DMA)

            overflow(pool, block_c)

            pool.wait_ge(y_complete, 1)
            pool.wait_ge(yrow_ready, 1)

            def tile_d(half, par):
                t = half * 2 + par
                pool.wait_ge(sum_done, t - 1 + CREDIT)
                nc.gpsimd.tensor_copy(slot_d[par][:, :], yrow[:, bass.ds(t * TOPK, TOPK)]).then_inc(slot_here, 1)
                pool.wait_ge(slot_here, t + 1)
                settle(pool)
                for k in range(TOPK):
                    nc.gpsimd.indirect_dma_start(
                        y4[par][:, k, :], None, y_dram,
                        bass.IndirectOffsetOnAxis(ap=slot_d[par][:, k:k + 1], axis=0)).then_inc(y4_gathered[par], DMA)

            outputs(pool, tile_d)

        @block.tensor
        def _(pe):
            for n in ("xs_done pv_done qk_done v_done ss_done av_done o_done logit_done rank_done").split():
                pe.sem_inc(sig[n], CREDIT)
            pe.wait_ge(const_ready, 1)

            def fill(t, name, mode, parts, *after):
                b, m = fill_of(t, name, mode)
                if not (isinstance(m, int) and m == 0):
                    pe.wait_ge(tp_copied[b], m)
                for s, v in after:
                    pe.wait_ge(s, v)
                for dst, src, size in parts(tp[b]):
                    last = nc.tensor.transpose(dst, src, ident[0:size, 0:size])
                last.then_inc(tp_full[b], 1)

            f = 0
            for n in range(4):
                pe.wait_ge(w_loaded[("wq", "wk", "wv", "wo")[n]], DMA)
                for dc in range(NC):
                    b, m = f % 2, f // 2
                    if m:
                        pe.wait_ge(tp_copied[b], m)
                    for ec in range(NC):
                        last = nc.tensor.transpose(tp[b][:, ec * P:(ec + 1) * P],
                                                   stage_w[n % 2][:, ec, dc * P:(dc + 1) * P], ident[:, :])
                    last.then_inc(tp_full[b], 1)
                    f += 1
            pe.wait_ge(w_loaded["gate"], DMA)
            for half in range(2):
                b, m = f % 2, f // 2
                pe.wait_ge(tp_copied[b], m)
                for j in range(2):
                    dc = half * 2 + j
                    last = nc.tensor.transpose(tp[b][:, j * E:(j + 1) * E], stage_g[:, dc * P:(dc + 1) * P],
                                               ident[0:E, 0:E])
                last.then_inc(tp_full[b], 1)
                f += 1
            assert f == WFILLS

            def turn_ctx(t, par, mode):
                for dc in range(NC):
                    fill(t, f"ctx{dc}", mode, lambda b: [
                        (b[:, c * P:(c + 1) * P], ctx_sb[:, par, c, dc * P:(dc + 1) * P], P) for c in range(MC)])

            def turn(src):
                return lambda b: [(b[:, c * P:(c + 1) * P], src[:, c * P:(c + 1) * P], P) for c in range(NC)]

            def mm4(dst, lhsT, rhs):
                for c in range(NC):
                    last = nc.tensor.matmul(dst, lhsT[:, c, :], rhs[:, c, :], start=(c == 0), stop=(c == NC - 1))
                return last

            def cross_scores(t, tt, mode):
                for name in ("ctx2", "ctx3", "xn1T"):
                    wait_copied(pe, t, name, mode)
                pe.wait_ge(sig["x1_done"], tt + CREDIT)
                mm4(xb[:, :], xn1T, ctxT).then_inc(sig["xs_done"], 1)

            def readout(t, tt, par, mode):
                wait_copied(pe, t, "xpT", mode)
                for c in range(MC):
                    last = nc.tensor.matmul(xb[:, :], xpT[:, c, :], ctx_sb[:, par, c, :], start=(c == 0),
                                            stop=(c == MC - 1))
                last.then_inc(sig["pv_done"], 1)

            def loaded(tt, half, par):
                pe.wait_ge(x_loaded[par], (half + 1) * (2 + BT) * DMA)

            loaded(0, 0, 0)
            turn_ctx(0, 0, "first")
            fill(0, "xn1T", "first", turn(xn1), (sig["ln1_done"], 1 + CREDIT))
            cross_scores(0, 0, "first")
            fill(0, "xpT", "first", turn(xp), (sig["xexp_done"], 1 + CREDIT))
            readout(0, 0, 0, "first")

            def step(half, par, mode):
                t = half * 2 + par
                tt = t + 1
                nhalf, npar = (half, 1) if par == 0 else (half + 1, 0)
                fill(t, "xn2T", mode, turn(xn2), (sig["ln2_done"], t + 1 + CREDIT))
                wait_copied(pe, t, "xn2T", mode)
                pe.wait_ge(sig["attnT_done"], t + CREDIT)
                pe.wait_ge(sig["x2_done"], t + CREDIT)
                for w, dst in (("wq", qo), ("wk", ko)):
                    for ec in range(NC):
                        for dc in range(NC):
                            last = nc.tensor.matmul(dst[:, ec * P:(ec + 1) * P], wT[w][:, dc, ec * P:(ec + 1) * P],
                                                    xn2T[:, dc, :], start=(dc == 0), stop=(dc == NC - 1))
                    last.then_inc(sig["qk_done"], 1)
                pe.wait_ge(sig["slot_done"], t + CREDIT)
                mm4(vl[:, :], xn2T, wT["wv"]).then_inc(sig["v_done"], 1)
                pe.wait_ge(sig["qT_done"], t + 1 + CREDIT)
                pe.wait_ge(sig["kT_done"], t + 1 + CREDIT)
                pe.wait_ge(sig["ssub_done"], t + CREDIT)
                for g in range(4):
                    if g >= 2:
                        pe.wait_ge(row_tile_done, 2 * t + g - 1)
                    r = slice(HD * g, HD * g + HD)
                    for h in range(g, H, 4):
                        a, at = place(h) // 8, place(h) % 8
                        for b in range(BT):
                            c = slice(b * S, (b + 1) * S)
                            last = nc.tensor.matmul(s2[c, a, at * S:(at + 1) * S], qT[r, h // 4, c],
                                                    kT[r, h // 4, c], start=True, stop=True)
                    if g < 2:
                        last.then_inc(row_tile_done, 1)
                last.then_inc(sig["ss_done"], 1)
                if mode != "last":
                    loaded(tt, nhalf, npar)
                    turn_ctx(t, npar, mode)
                    fill(t, "xn1T", mode, turn(xn1), (sig["ln1_done"], tt + 1 + CREDIT))
                    cross_scores(t, tt, mode)
                for j in range(2):
                    fill(t, f"pT{j}", mode, lambda b: [
                        (b[:, c * P:(c + 1) * P], sp_sb[:, 8 * j + 2 * c:8 * j + 2 * c + 2, :], P) for c in range(4)],
                        (sig["sp_done"], t + 1 + CREDIT))
                wait_copied(pe, t, "pT0", mode)
                wait_copied(pe, t, "pT1", mode)
                pe.wait_ge(sig["vsb_done"], t + 1 + CREDIT)
                pe.wait_ge(swap_done, (t + 1) * (2 * DMA) + CREDIT * DMA)
                settle(pe)
                for h in range(H):
                    hh, j = place(h) % 2, place(h) // 2
                    for b in range(BT):
                        src = v_sb if hh == b else v_swap
                        at = (h // 8) * P + b * S
                        last = nc.tensor.matmul(
                            (qo, ko)[hh][HD * (h % 4):HD * (h % 4) + HD, at:at + S],
                            src[hh * S:(hh + 1) * S, h * HD:(h + 1) * HD],
                            pT[hh * S:(hh + 1) * S, j, b * S:(b + 1) * S], start=True, stop=True)
                last.then_inc(sig["av_done"], 1)
                if mode != "last":
                    fill(t, "xpT", mode, turn(xp), (sig["xexp_done"], tt + 1 + CREDIT))
                pe.wait_ge(sig["attnT_done"], t + 1 + CREDIT)
                mm4(ko[:, :], attnT, wT["wo"]).then_inc(sig["o_done"], 1)
                if mode != "last":
                    readout(t, tt, npar, mode)
                fill(t, "xn3T", mode, turn(xn3[:, par, :]), (sig["ln3_done"], t + 1 + CREDIT))
                wait_copied(pe, t, "xn3T", mode)
                mm4(vl[:, 0:E], xn3T, gateT).then_inc(sig["logit_done"], 1)
                pe.wait_ge(sig["sel_done"], t + 1 + CREDIT)
                nc.tensor.matmul(vl[:, E:2 * E], tri[:, :], sel[:, :], start=True, stop=True)
                nc.tensor.matmul(vl[:, 2 * E:3 * E], ones[:, :], sel[:, :], start=True,
                                 stop=True).then_inc(sig["rank_done"], 1)

            with pe.Fori(0, T // 2 - 1) as i:
                step(i, 0, "loop")
                step(i, 1, "loop")
            step(T // 2 - 1, 0, "loop")
            step(T // 2 - 1, 1, "last")

            for n, c in (("xT_full", 1), ("gu_done", 3), ("y0_full", 1), ("y1_full", 1)):
                pe.sem_inc(sg[n], c * CREDIT)

            def turn_rows(x):
                pe.wait_ge(gathered[x.par], (x.half + 1) * (2 * DMA))
                pe.wait_ge(sg["xlo_done"], x.e + CREDIT)
                for c in range(NC):
                    o = (c % 2) * CAP
                    nc.tensor.transpose(tp[c // 2][:, o:o + P], xg[x.par][:, 0, c::NC], ident[:, :])
                    last = nc.tensor.transpose(tp[c // 2][:, o + P:o + CAP], xg[x.par][0:CAP2, 1, c::NC],
                                               ident[0:CAP2, 0:CAP2])
                last.then_inc(sg["xT_full"], 1)

            PARTS = ((0, 0), (1, 0), (0, 1))

            def gate_up(x):
                pe.wait_ge(sg["xlo_done"], x.e + 1 + CREDIT)
                pe.wait_ge(sg["wlo_done"], x.e + 1 + CREDIT)
                w, cw, xs = gu[x.par], cgu[x.pair_par], xT[x.par]
                parts = [[lambda p, c, s=s: w[p][:, c, s * P:(s + 1) * P] for s in range(2)],
                         [lambda p, c: w[p][:, c, 2 * P:3 * P]],
                         [lambda p, c, s=s: cw[p][:, s, c, :] for s in range(2)]]
                for j, group in enumerate(parts):
                    pe.wait_ge(sg["mul_done"], x.e * 3 + (j + 1 + 3 * CREDIT - 3))
                    for s, lhsT in enumerate(group):
                        dst = g_bank[j][:, s * CAP:(s + 1) * CAP]
                        for c in range(NC):
                            for n, (pw, px) in enumerate(PARTS):
                                last = nc.tensor.matmul(dst, lhsT(pw, c), xs[px][:, c, :],
                                                        start=(c == 0 and n == 0), stop=(c == NC - 1 and n == 2))
                    last.then_inc(sg["gu_done"], 1)

            def down(x):
                pe.wait_ge(sg["alo_done"], x.e + 1 + CREDIT)
                pe.wait_ge(sg["dlo_done"], x.e + 1 + CREDIT)
                a, w, cw = aT[x.par], dn[x.par], cdn[x.pair_par]
                for blk, full in ((0, "y0"), (1, "y1")):
                    pe.wait_ge(sg[f"{full}_done"], x.e + CREDIT)
                    for k in range(3):
                        for n, (pa, pw) in enumerate(PARTS):
                            rhs = w[pw][:, k, :] if k < 2 else cw[pw][:, :]
                            last = nc.tensor.matmul(y_bank[blk][:, :], a[pa][:, k, blk * CAP2:blk * CAP2 + P], rhs,
                                                    start=(k == 0 and n == 0), stop=(k == 2 and n == 2))
                    last.then_inc(sg[f"{full}_full"], 1)

            turn_rows(Expert(0, 0))

            def step(x):
                if x.ahead(1) is not None:
                    turn_rows(x.ahead(1))
                gate_up(x)
                if x.ahead(-1) is not None:
                    down(x.ahead(-1))

            experts(pe, step)
            down(Expert(E // 4 - 1, 3))

            def block_c(k):
                pe.wait_ge(sv["c_gathered"], (k + 1) * DMA)
                for c in range(NC):
                    last = nc.tensor.transpose(tp[0][:, c * P:(c + 1) * P], xg[0][:, 0, c::NC], ident[:, :])
                last.then_inc(sv["c_xT_full"], 1)
                pe.wait_ge(sv["c_xT_done"], k + 1)
                pe.wait_ge(sv["c_w_loaded"], (k + 1) * (7 * DMA))
                for j in range(3):
                    for s in range(1 if j == 1 else 2):
                        for c in range(NC):
                            o = 2 * P if j else s * P
                            lhsT = raw_gu[0][:, c, o:o + P] if j < 2 else raw_c[:, s, c, :]
                            last = nc.tensor.matmul(g_bank[j][:, s * P:(s + 1) * P], lhsT, xn1T[:, c, :],
                                                    start=(c == 0), stop=(c == NC - 1))
                last.then_inc(sv["c_gu_done"], 1)
                pe.wait_ge(sv["c_mul_done"], k + 1)
                for j in range(3):
                    rhs = raw_d[0][:, j, :] if j < 2 else raw_cd
                    last = nc.tensor.matmul(y_bank[0][:, :], act_a[:, j, 0:P], rhs, start=(j == 0), stop=(j == 2))
                last.then_inc(sv["c_y_full"], 1)

            overflow(pe, block_c)

        @block.scalar
        def _(act):
            for n in "xexp_done qT_done vsb_done sexp_done lexp_done".split():
                act.sem_inc(sig[n], CREDIT)
            copy = nc.scalar.copy

            for f in range(0, WFILLS, 2):
                act.wait_ge(tp_full[0], f // 2 + 1)
                if f < 16:
                    copy(wT[("wq", "wk", "wv", "wo")[f // 4]][:, f % 4, :], tp[0]).then_inc(tp_copied[0], 1)
                else:
                    copy(gateT[:, 0:2, :], chunks(tp[0][:, 0:2 * E], E)).then_inc(tp_copied[0], 1)

            def cp(t, name, mode, dst, *after):
                b, m = fill_of(t, name, mode)
                act.wait_ge(tp_full[b], m + 1)
                for s, v in after:
                    act.wait_ge(s, v)
                copy(dst, chunks(tp[b], P)).then_inc(tp_copied[b], 1)

            def ctx_part(t, tt, mode):
                b0 = ((sig["xs_done"], tt + CREDIT),)
                for dc in (0, 2):
                    cp(t, f"ctx{dc}", mode, chunks(ctxT[:, dc, :], P), *b0)
                cp(t, "xn1T", mode, xn1T[:, :, :], *b0)

            def cross_exp(tt):
                act.wait_ge(sig["xmax_done"], tt + 1 + CREDIT)
                act.wait_ge(sig["xrv_done"], tt + CREDIT)
                for b in range(BT):
                    r = slice(b * S, (b + 1) * S)
                    last = nc.scalar.activation(xp[r, b * M:(b + 1) * M], xsc[r, :], ACT.Exp, bias=xnb[r, :],
                                                scale=XS_SCALE, accum_out=xsum[r, :])
                last.then_inc(sig["xexp_done"], 1)

            act.wait_ge(const_ready, 1)
            act.wait_ge(dve_const, 1)
            ctx_part(0, 0, "first")
            cross_exp(0)
            cp(0, "xpT", "first", xpT[:, :, :], (sig["pv_done"], CREDIT))

            def body(t, par, mode):
                tt = t + 1
                cp(t, "xn2T", mode, xn2T[:, :, :], (sig["v_done"], t + CREDIT))
                act.wait_ge(sig["qk_done"], t * 2 + 1 + CREDIT)
                act.wait_ge(sig["ss_done"], t + CREDIT)
                copy(qT[:, :, :], chunks(qo[:, :], P)).then_inc(sig["qT_done"], 1)
                act.wait_ge(sig["v_done"], t + 1 + CREDIT)
                act.wait_ge(sig["av_done"], t + CREDIT)
                act.wait_ge(swap_done, t * (2 * DMA) + CREDIT * DMA)
                copy(v_sb[:, :], vl[:, :]).then_inc(sig["vsb_done"], 1)
                if mode != "last":
                    ctx_part(t, tt, mode)
                act.wait_ge(sig["ssub_done"], t + 1 + CREDIT)
                nc.scalar.activation(sp_sb[:, :, :], sp_sb[:, :, :], ACT.Exp, scale=SS_SCALE).then_inc(
                    sig["sexp_done"], 1)
                if mode != "last":
                    cross_exp(tt)
                cp(t, "pT0", mode, pT[:, 0:4, :], (sig["av_done"], t + CREDIT))
                if mode != "last":
                    cp(t, "xpT", mode, xpT[:, :, :], (sig["pv_done"], tt + CREDIT))
                cp(t, "xn3T", mode, xn3T[:, :, :], (sig["logit_done"], t + CREDIT))
                act.wait_ge(sig["lmax_done"], t + 1 + CREDIT)
                nc.scalar.activation(enl[:, :], logit[:, :], ACT.Exp, scale=-1.0)
                nc.scalar.activation(el[:, :], logit[:, :], ACT.Exp, bias=lmax[:, :]).then_inc(sig["lexp_done"], 1)

            tiles(act, body)

            for n, c in (("xhi_done", 1), ("whi_done", 1), ("silu_done", 2), ("dhi_done", 1), ("ahi_done", 1),
                         ("y0_done", 1)):
                act.sem_inc(sg[n], c * CREDIT)

            def rows_hi(x):
                act.wait_ge(sg["xT_full"], x.e + 1 + CREDIT)
                act.wait_ge(sg["gu_done"], (x.e - 1 + CREDIT) * 3)
                copy(xT[x.par][0][:, :, :].rearrange("p (a c) n -> p a (c n)", a=2),
                     tpair[:, :, 0:2 * CAP]).then_inc(sg["xhi_done"], 1)

            def gu_hi(x):
                act.wait_ge(gu_loaded[x.par], (x.half + 1) * (2 * DMA))
                last = copy(gu[x.par][0][:, :, :], raw_gu[x.par])
                if x.first_of_pair:
                    act.wait_ge(c_loaded, (x.half + 1) * (2 * DMA))
                    last = copy(cgu[x.pair_par][0][:, :, :, :], raw_c)
                last.then_inc(sg["whi_done"], 1)

            def silu_large(n):
                nc.scalar.activation(act_g[F2:P, 1, 0:n], g_bank[0][0:F2, 0:n], ACT.Silu)
                nc.scalar.activation(act_g[0:F2, 0, 0:n], g_bank[0][F2:P, 0:n], ACT.Silu)
                return nc.scalar.activation(act_g[F2:P, 0, 0:n], g_bank[0][0:F2, n:2 * n], ACT.Silu)

            def silu(x):
                act.wait_ge(sg["gu_done"], (x.e + CREDIT) * 3 + 1)
                act.wait_ge(sg["mul_done"], (x.e + CREDIT) * 3)
                silu_large(CAP).then_inc(sg["silu_done"], 1)
                act.wait_ge(sg["gu_done"], (x.e + CREDIT) * 3 + 3)
                nc.scalar.activation(act_g[:, 2, :], g_bank[2][:, 0:CAP], ACT.Silu).then_inc(sg["silu_done"], 1)

            def d_hi(x):
                act.wait_ge(d_loaded[x.par], (x.half + 1) * (2 * DMA))
                act.wait_ge(sg["y1_full"], x.e - 1 + CREDIT)
                last = copy(dn[x.par][0][:, :, :], raw_d[x.par])
                if x.first_of_pair:
                    act.wait_ge(cd_loaded, (x.half + 1) * DMA)
                    last = copy(cdn[x.pair_par][0][:, :], raw_cd)
                last.then_inc(sg["dhi_done"], 1)

            def a_hi(x):
                act.wait_ge(sg["mul_done"], (x.e + CREDIT) * 3 + 3)
                copy(aT[x.par][0][:, :, :], act_a).then_inc(sg["ahi_done"], 1)

            def y_out(x):
                act.wait_ge(sg["y0_full"], x.e + 1 + CREDIT)
                act.wait_ge(y_stored[x.par], x.half * (2 * DMA) + 2 * CREDIT * DMA)
                copy(y_sb[x.par][:, 0, :], y_bank[0][:, :]).then_inc(sg["y0_done"], 1)

            rows_hi(Expert(0, 0))
            gu_hi(Expert(0, 0))

            def step(x):
                if x.ahead(1) is not None:
                    rows_hi(x.ahead(1))
                    gu_hi(x.ahead(1))
                silu(x)
                d_hi(x)
                a_hi(x)
                if x.ahead(-1) is not None:
                    y_out(x.ahead(-1))

            act.wait_ge(pads_zero, 1)
            experts(act, step)
            y_out(Expert(E // 4 - 1, 3))

            def block_c(k):
                act.wait_ge(sv["c_gu_done"], k + 1)
                silu_large(P)
                nc.scalar.activation(act_g[:, 2, 0:P], g_bank[2][:, 0:P], ACT.Silu).then_inc(sv["c_silu_done"], 1)

            overflow(act, block_c)

        @block.vector
        def _(dve):
            v = nc.vector
            for n in ("ln1_var ln1_done xmax_done xrv_done x1_done ln2_var ln2_done kT_done ssub_done sp_done "
                      "attnT_done x2_done ln3_var ln3_done lmax_done sel_done slot_done").split():
                dve.sem_inc(sig[n], CREDIT)

            class Chain:
                base, k = 0, 0

                def __call__(self, instruction):
                    self.k += 1
                    instruction.then_inc(dve_chain, 1)
                    dve.wait_ge(dve_chain, self.base + self.k)

            link = Chain()
            v.memset(xp[:, :], 0.0).then_inc(dve_const, 1)

            for f in range(1, WFILLS, 2):
                dve.wait_ge(tp_full[1], f // 2 + 1)
                if f < 16:
                    v.tensor_copy(wT[("wq", "wk", "wv", "wo")[f // 4]][:, f % 4, :], tp[1]).then_inc(tp_copied[1], 1)
                else:
                    v.tensor_copy(gateT[:, 2:4, :], chunks(tp[1][:, 0:2 * E], E)).then_inc(tp_copied[1], 1)
            dve.wait_ge(const_ready, 1)
            link(v.tensor_copy(run[:, :], base_e[:, :]))

            def norm_stats(col, src, n):
                link(v.bn_stats(stat[:, col, :], src))
                settle(dve)
                link(v.bn_aggr(mv[:, col, :], stat[:, col, :]))
                v.tensor_scalar_add(vare[:, col:col + 1], mv[:, col, 1:2], EPS).then_inc(sig[f"{n}_var"], 1)

            def norm_apply(col, src, dst, n, t):
                dve.wait_ge(sig[f"{n}_rstd"], t + 1 + CREDIT)
                v.tensor_scalar(dst, src, mv[:, col, 0:1], rstd[:, col:col + 1], ALU.subtract,
                                ALU.mult).then_inc(sig[f"{n}_done"], 1)

            def cp(t, name, mode, dst, *after):
                b, m = fill_of(t, name, mode)
                dve.wait_ge(tp_full[b], m + 1)
                for s, val in after:
                    dve.wait_ge(s, val)
                v.tensor_copy(dst, chunks(tp[b], P)).then_inc(tp_copied[b], 1)

            def ctx_part(t, tt, mode):
                for dc in (1, 3):
                    cp(t, f"ctx{dc}", mode, chunks(ctxT[:, dc, :], P), (sig["xs_done"], tt + CREDIT))

            def first_norm(tt, half, par):
                dve.wait_ge(x_loaded[par], (half + 1) * (2 + BT) * DMA)
                norm_stats(0, x_in[:, par, :], "ln1")
                link(v.tensor_scalar(maskb[:, :], mask_u8[:, par, :], 1.0, NEG, ALU.subtract, ALU.mult))
                link(v.tensor_reduce(valid[:, :], mask_u8[:, par, :], AX.X, ALU.max))
                norm_apply(0, x_in[:, par, :], xn1[:, :], "ln1", tt)

            def cross_max(tt):
                dve.wait_ge(sig["xs_done"], tt + 1 + CREDIT)
                dve.wait_ge(sig["xexp_done"], tt + CREDIT)
                settle(dve)
                for b in range(BT):
                    r = slice(b * S, (b + 1) * S)
                    last = v.tensor_tensor_reduce(out=xsc[r, :], in0=xb[r, b * M:(b + 1) * M], in1=maskb[r, :],
                                                  scale=1.0, scalar=-3.0e38, op0=ALU.add, op1=ALU.max,
                                                  accum_out=xmax[r, :])
                link(last)
                v.tensor_scalar(xnb[:, :], xmax[:, :], -XS_SCALE, None, ALU.mult).then_inc(sig["xmax_done"], 1)

            def cross_sum(tt):
                dve.wait_ge(sig["xexp_done"], tt + 1 + CREDIT)
                link(v.reciprocal(xrs[:, :], xsum[:, :]))
                v.tensor_tensor(xrv[:, :], xrs[:, :], valid[:, :], ALU.mult).then_inc(sig["xrv_done"], 1)

            def residual1(tt, par):
                dve.wait_ge(sig["pv_done"], tt + 1 + CREDIT)
                dve.wait_ge(sig["xrv_done"], tt + 1 + CREDIT)
                v.scalar_tensor_tensor(out=x1[:, :], in0=xb[:, :], scalar=xrv[:, :], in1=x_in[:, par, :],
                                       op0=ALU.mult, op1=ALU.add).then_inc(sig["x1_done"], 1)
                dve.wait_ge(sig["x1_done"], tt + 1 + CREDIT)
                norm_stats(1, x1[:, :], "ln2")
                norm_apply(1, x1[:, :], xn2[:, :], "ln2", tt)

            first_norm(0, 0, 0)
            ctx_part(0, 0, "first")
            cross_max(0)
            cross_sum(0)
            residual1(0, 0)

            def step(half, par, mode):
                t = half * 2 + par
                tt = t + 1
                nhalf, npar = (half, 1) if par == 0 else (half + 1, 0)
                if mode != "last":
                    first_norm(tt, nhalf, npar)
                dve.wait_ge(sig["qk_done"], t * 2 + 2 + CREDIT)
                dve.wait_ge(sig["ss_done"], t + CREDIT)
                v.tensor_copy(kT[:, :, :], chunks(ko[:, :], P)).then_inc(sig["kT_done"], 1)
                dve.wait_ge(sig["ss_done"], t + 1 + CREDIT)
                s3 = s2[:, :, :].rearrange("p a (h k) -> p (a h) k", k=S)
                link(v.tensor_reduce(smax[:, :], s3, AX.X, ALU.max))
                v.tensor_tensor(sp_sb[:, :, :], s3, spread(smax[:, :], 2, S), ALU.subtract).then_inc(
                    sig["ssub_done"], 1)
                if mode != "last":
                    ctx_part(t, tt, mode)
                dve.wait_ge(sig["sexp_done"], t + 1 + CREDIT)
                link(v.tensor_reduce(ssum[:, :], sp_sb[:, :, :], AX.X, ALU.add))
                link(v.reciprocal(srec[:, :], ssum[:, :]))
                v.tensor_tensor(sp_sb[:, :, :], sp_sb[:, :, :], spread(srec[:, :], 2, S), ALU.mult).then_inc(
                    sig["sp_done"], 1)
                if mode != "last":
                    cross_max(tt)
                cp(t, "pT1", mode, pT[:, 4:8, :], (sig["av_done"], t + CREDIT))
                if mode != "last":
                    cross_sum(tt)
                dve.wait_ge(sig["av_done"], t + 1 + CREDIT)
                dve.wait_ge(sig["o_done"], t + CREDIT)
                for half_of, src in ((0, qo), (1, ko)):
                    last = v.tensor_copy(attnT[:, :, :].rearrange("p (c two) q -> p two c q", two=2)[:, half_of],
                                         chunks(src[:, 0:2 * P], P))
                last.then_inc(sig["attnT_done"], 1)
                dve.wait_ge(sig["o_done"], t + 1 + CREDIT)
                dve.wait_ge(x2_stored[par], (half + CREDIT) * DMA)
                v.tensor_tensor(x2[:, par, :], ko[:, :], x1[:, :], ALU.add).then_inc(sig["x2_done"], 1)
                dve.wait_ge(sig["x2_done"], t + 1 + CREDIT)
                norm_stats(2, x2[:, par, :], "ln3")
                dve.wait_ge(xn_stored[par], (half + CREDIT) * DMA)
                norm_apply(2, x2[:, par, :], xn3[:, par, :], "ln3", t)
                if mode != "last":
                    residual1(tt, npar)
                dve.wait_ge(sig["logit_done"], t + 1 + CREDIT)
                link(v.tensor_copy(logit[:, :], vl[:, 0:E]))
                v.tensor_reduce(lmax[:, :], logit[:, :], AX.X, ALU.max, negate=True).then_inc(sig["lmax_done"], 1)
                dve.wait_ge(sig["lexp_done"], t + 1 + CREDIT)
                link(v.tensor_scalar_add(sg1[:, :], enl[:, :], 1.0))
                link(v.reciprocal(score[:, :], sg1[:, :]))
                settle(dve)
                link(v.max(top8[:, :], score[:, :]))
                settle(dve)
                link(v.max_index(idx8[:, :], top8[:, :], score[:, :]))
                link(v.tensor_copy(idxf[:, :], idx8[:, 0:TOPK]))
                link(v.tensor_tensor(hot[:, :, :], spread(iota_e[:, :], 1, TOPK), spread(idxf[:, :], 2, E),
                                     ALU.is_equal))
                with nc.allow_low_precision(reason="zeros and ones"):
                    v.tensor_reduce(sel[:, :], hot[:, :, :].rearrange("p k e -> p e k"), AX.X, ALU.add).then_inc(
                        sig["sel_done"], 1)
                link(v.tensor_tensor(prod[:, :, :], hot[:, :, :], spread(el[:, :], 1, TOPK), ALU.mult))
                link(v.tensor_reduce(wraw[:, :], prod[:, :, :], AX.X, ALU.add))
                link(v.tensor_reduce(wsum[:, :], wraw[:, :], AX.X, ALU.add))
                link(v.reciprocal(wrec[:, :], wsum[:, :]))
                dve.wait_ge(slots_used, t - 1 + CREDIT)
                link(v.tensor_scalar(wn[:, :], wraw[:, :], wrec[:, :], None, ALU.mult))
                v.tensor_copy(w_all[:, bass.ds(t * TOPK, TOPK)], wn[:, :])
                v.tensor_copy(e_all[:, bass.ds(t * TOPK, TOPK)], idxf[:, :])
                v.tensor_copy(tok[:, par, :], tokf[:, :])
                dve.wait_ge(sig["rank_done"], t + 1 + CREDIT)
                link(v.tensor_tensor(slotb[:, :], vl[:, E:2 * E], run[:, :], ALU.add))
                link(v.tensor_tensor(prod2[:, :, :], hot[:, :, :], spread(slotb[:, :], 1, TOPK), ALU.mult))
                link(v.tensor_reduce(slotf[:, :], prod2[:, :, :], AX.X, ALU.add))
                link(v.tensor_scalar_add(tokf[:, :], tokf[:, :], float(P)))
                link(v.tensor_tensor(run[:, :], vl[:, 2 * E:3 * E], run[:, :], ALU.add))
                v.tensor_copy(s_all[:, bass.ds(t * TOPK, TOPK)], slotf[:, :])
                v.tensor_copy(slot[:, par, :], slotf[:, :]).then_inc(sig["slot_done"], 1)
                dve.wait_ge(sig["slot_done"], t + 1 + CREDIT)

            first = link.k
            per_step = LINKS
            with dve.Fori(0, T // 2 - 1) as i:
                link.base, link.k = i * (2 * per_step) + first, 0
                step(i, 0, "loop")
                assert link.k == per_step, link.k
                step(i, 1, "loop")
            link.base, link.k = first + 2 * per_step * (T // 2 - 1), 0
            step(T // 2 - 1, 0, "loop")
            step(T // 2 - 1, 1, "last")
            count = first + per_step * (T - 2) + link.k
            link.base, link.k = count, 0

            for n, c in (("xlo_done", 1), ("wlo_done", 1), ("mul_done", 3), ("dlo_done", 1), ("alo_done", 1),
                         ("y1_done", 1)):
                dve.sem_inc(sg[n], c * CREDIT)
            dve.wait_ge(sig["o_done"], T + CREDIT)
            for n in range(2):
                v.memset(raw_d[n][0:P - F2, 1, :], 0.0)
            link(v.memset(act_a[0:P - F2, 1, :], 0.0))
            dve.sem_inc(pads_zero, 1)

            link(v.tensor_tensor(cnt[:, :], run[:, :], base_e[:, :], ALU.subtract))
            link(v.tensor_tensor(sc[:, 0:OVB, :], spread(cnt[:, :], 1, OVB), spread(thr[:, :], 2, E), ALU.is_gt))
            link(v.tensor_reduce(nblk[:, :], sc[:, 0:OVB, :].rearrange("p a b -> p b a"), AX.X, ALU.add))
            link(v.tensor_tensor(sc[:, :, :], lower[:, :, :], spread(nblk[:, :], 1, E), ALU.mult))
            link(v.tensor_reduce(cum[:, :], sc[:, :, :], AX.X, ALU.add))
            link(v.tensor_tensor(before[:, :], cum[:, :], nblk[:, :], ALU.subtract))
            meta_sc, meta_sc2 = sc[0:1, 0:KMAX, :], sc2[0:1, 0:KMAX, :]
            link(v.tensor_tensor(meta_sc, spread(cum[0:1, :], 1, KMAX), spread(ordi[:, :], 2, E), ALU.is_le))
            link(v.tensor_reduce(meta_f[:, 1, :], meta_sc, AX.X, ALU.add))
            link(v.tensor_tensor(meta_sc2, meta_sc, spread(nblk[0:1, :], 1, KMAX), ALU.mult))
            link(v.tensor_reduce(meta_f[:, 2, :], meta_sc2, AX.X, ALU.add))
            link(v.tensor_tensor(meta_f[:, 3, :], ordi[:, :], meta_f[:, 2, :], ALU.subtract))
            link(v.tensor_scalar(meta_f[:, 2, :], meta_f[:, 3, :], float(P), float(CAP), ALU.mult, ALU.add))
            link(v.scalar_tensor_tensor(out=meta_f[:, 3, :], in0=meta_f[:, 1, :], scalar=float(REGION),
                                        in1=meta_f[:, 2, :], op0=ALU.mult, op1=ALU.add))
            link(v.tensor_copy(meta_f[:, 0, :], cum[0:1, E - 1:E].broadcast_to([1, KMAX])))
            link(v.tensor_copy(meta_i[:, :, :], meta_f[:, :, :]))
            link(v.tensor_scalar(meta_half[:, :], meta_i[:, 1, :], 1, None, ALU.logical_shift_right))
            link(v.tensor_copy(meta_i[:, 2, :], meta_half[:, :]))
            dve.sem_inc(meta_ready, 1)
            link(v.tensor_tensor(sc[:, :, :], spread(iota_e[:, :], 1, T * TOPK), spread(e_all[:, :], 2, E), ALU.is_equal))
            link(v.tensor_tensor(sc2[:, :, :], sc[:, :, :], spread(before[:, :], 1, T * TOPK), ALU.mult))
            link(v.tensor_reduce(over[:, :], sc2[:, :, :], AX.X, ALU.add))
            link(v.scalar_tensor_tensor(out=rank[:, :], in0=e_all[:, :], scalar=-float(REGION), in1=s_all[:, :],
                                        op0=ALU.mult, op1=ALU.add))
            link(v.tensor_scalar(past[:, :], rank[:, :], float(CAP), None, ALU.is_ge))
            link(v.scalar_tensor_tensor(out=over[:, :], in0=e_all[:, :], scalar=-float(CAP) / P, in1=over[:, :],
                                        op0=ALU.mult, op1=ALU.add))
            link(v.tensor_scalar(over[:, :], over[:, :], float(P), float((E - 1) * CAP), ALU.mult, ALU.add))
            link(v.tensor_tensor(over[:, :], over[:, :], past[:, :], ALU.mult))
            link(v.scalar_tensor_tensor(out=rank[:, :], in0=e_all[:, :], scalar=float(CAP), in1=rank[:, :],
                                        op0=ALU.mult, op1=ALU.add))
            link(v.tensor_tensor(rank[:, :], rank[:, :], over[:, :], ALU.add))
            v.tensor_copy(yrow[:, :], rank[:, :]).then_inc(yrow_ready, 1)

            def plain(ap):
                return ap.bitcast(F32)

            def lo(parts, src, dst_of=lambda t: t[:]):
                return v.tensor_tensor(dst_of(parts[1]), src, plain(dst_of(parts[0])), ALU.subtract)

            def rows_lo(x):
                dve.wait_ge(sg["xhi_done"], x.e + 1 + CREDIT)
                lo(xT[x.par], tpair[:, :, 0:2 * CAP], lambda t: t[:, :, :].rearrange(
                    "p (a c) n -> p a (c n)", a=2)).then_inc(sg["xlo_done"], 1)

            def gu_lo(x):
                dve.wait_ge(sg["whi_done"], x.e + 1 + CREDIT)
                last = lo(gu[x.par], raw_gu[x.par], lambda t: t[:, :, :])
                if x.first_of_pair:
                    last = lo(cgu[x.pair_par], raw_c, lambda t: t[:, :, :, :])
                last.then_inc(sg["wlo_done"], 1)

            def multiply(x):
                dve.wait_ge(sg["alo_done"], x.e + CREDIT)
                dve.wait_ge(sg["silu_done"], (x.e + CREDIT) * 2 + 1)
                v.tensor_tensor(act_a[F2:P, 1, :], act_g[F2:P, 1, :], g_bank[0][F2:P, CAP:2 * CAP],
                                ALU.mult).then_inc(sg["mul_done"], 1)
                dve.wait_ge(sg["gu_done"], (x.e + CREDIT) * 3 + 2)
                v.tensor_tensor(act_a[:, 0, :], act_g[:, 0, :], g_bank[1][:, 0:CAP], ALU.mult).then_inc(
                    sg["mul_done"], 1)
                dve.wait_ge(sg["silu_done"], (x.e + CREDIT) * 2 + 2)
                v.scalar_tensor_tensor(out=act_a[:, 2, :], in0=act_g[:, 2, :], scalar=SMALL_SCALE,
                                       in1=g_bank[2][:, CAP:2 * CAP], op0=ALU.mult, op1=ALU.mult).then_inc(
                                           sg["mul_done"], 1)

            def d_lo(x):
                dve.wait_ge(sg["dhi_done"], x.e + 1 + CREDIT)
                last = lo(dn[x.par], raw_d[x.par], lambda t: t[:, :, :])
                if x.first_of_pair:
                    last = lo(cdn[x.pair_par], raw_cd, lambda t: t[:, :])
                last.then_inc(sg["dlo_done"], 1)

            def a_lo(x):
                dve.wait_ge(sg["ahi_done"], x.e + 1 + CREDIT)
                lo(aT[x.par], act_a, lambda t: t[:, :, :]).then_inc(sg["alo_done"], 1)

            def y_out(x):
                dve.wait_ge(sg["y1_full"], x.e + 1 + CREDIT)
                dve.wait_ge(y_stored[x.par], x.half * (2 * DMA) + 2 * CREDIT * DMA)
                v.tensor_copy(y_sb[x.par][:, 1, :], y_bank[1][:, :]).then_inc(sg["y1_done"], 1)

            rows_lo(Expert(0, 0))
            gu_lo(Expert(0, 0))

            def step(x):
                if x.ahead(1) is not None:
                    rows_lo(x.ahead(1))
                    gu_lo(x.ahead(1))
                multiply(x)
                d_lo(x)
                a_lo(x)
                if x.ahead(-1) is not None:
                    y_out(x.ahead(-1))

            experts(dve, step)
            y_out(Expert(E // 4 - 1, 3))


            def block_c(k):
                dve.wait_ge(sv["c_xT_full"], k + 1)
                v.tensor_copy(xn1T[:, :, :], chunks(tp[0], P)).then_inc(sv["c_xT_done"], 1)
                dve.wait_ge(sv["c_silu_done"], k + 1)
                v.tensor_tensor(act_a[:, 0, 0:P], act_g[:, 0, 0:P], g_bank[1][:, 0:P], ALU.mult)
                v.tensor_tensor(act_a[F2:P, 1, 0:P], act_g[F2:P, 1, 0:P], g_bank[0][F2:P, P:2 * P], ALU.mult)
                v.scalar_tensor_tensor(out=act_a[:, 2, 0:P], in0=act_g[:, 2, 0:P], scalar=SMALL_SCALE,
                                       in1=g_bank[2][:, P:2 * P], op0=ALU.mult, op1=ALU.mult).then_inc(
                                           sv["c_mul_done"], 1)
                dve.wait_ge(sv["c_y_full"], k + 1)
                v.tensor_copy(y_sb[0][:, 0, :], y_bank[0][:, :]).then_inc(sv["c_y_done"], 1)

            overflow(dve, block_c)

            dve.sem_inc(sum_done, CREDIT)
            base = link.base + link.k

            def tile_d(half, par):
                t = half * 2 + par
                dve.wait_ge(d_loaded_t[par], (half + 1) * DMA)
                link(v.tensor_copy(w_d[par][:, :], w_all[:, bass.ds(t * TOPK, TOPK)]))
                dve.wait_ge(y4_gathered[par], (half + 1) * (TOPK * DMA))
                dve.wait_ge(out_stored[par], (half + CREDIT) * DMA)
                for k in range(TOPK):
                    acc = x_in[:, par, :] if k == 0 else x2[:, par, :]
                    ins = v.scalar_tensor_tensor(out=x2[:, par, :], in0=y4[par][:, k, :], scalar=w_d[par][:, k:k + 1],
                                                 in1=acc, op0=ALU.mult, op1=ALU.add)
                    if k < TOPK - 1:
                        link(ins)
                ins.then_inc(sum_done, 1)

            with dve.Fori(0, T // 2) as i:
                link.base, link.k = i * (2 * TOPK) + base, 0
                for par in range(2):
                    tile_d(i, par)


_INS = ['x', 'ctx_2048', 'mask_BxS2_bk0', 'L0_attn_w_q', 'L0_attn_w_k', 'L0_attn_w_v', 'L0_attn_w_o', 'L0_ffn_gate_w',
        'L0_ffn_Wg', 'L0_ffn_Wu', 'L0_ffn_Wd', 'L0_ffn_cWg', 'L0_ffn_cWu', 'L0_ffn_cWd']


def kernel(**inputs):
    import numpy as _np
    import concourse.bacc as _bacc
    from concourse import mybir as _mybir
    from concourse.bass_utils import run_bass_kernel_spmd as _run

    nc = _bacc.Bacc("TRN2", target_bir_lowering=False, num_devices=1)
    arrays, args = {}, []
    for name in _INS:
        a = _np.ascontiguousarray(inputs[name])
        if a.dtype.kind == "b":
            a = a.view(_np.uint32)
        arrays[f"in_{name}_dram"] = a
        args.append(nc.dram_tensor(f"in_{name}_dram", a.shape, _mybir.dt.from_np(a.dtype), kind="ExternalInput").ap())
    shape = inputs['x'].shape
    args.append(nc.dram_tensor("out_0_dram", shape, _mybir.dt.from_np(_np.dtype("float32")), kind="ExternalOutput").ap())
    perceiver_moe(nc, *args)
    r = _run(nc, [arrays], core_ids=[0])
    return r.results[0]["out_0_dram"]
```

```python
from contextlib import ExitStack

import concourse.bass as bass
from concourse import mybir

F32 = mybir.dt.float32
F32R = mybir.dt.float32r
BF16 = mybir.dt.bfloat16
I32 = mybir.dt.int32
U32 = mybir.dt.uint32
U8 = mybir.dt.uint8
ALU = mybir.AluOpType
ACT = mybir.ActivationFunctionType
AX = mybir.AxisListType

P = 128
CREDIT = 2
DMA = 16
CAP = 208
EPS = 1e-5
NEG = 1e30
LOWEST = -88.0
SMALL_SCALE = 0.05
LINKS = 33


def most_blocks(experts, tokens, choices):
    best = {0: 0}
    for _ in range(experts):
        new = dict(best)
        for blocks, used in best.items():
            for m in range(1, -(-(tokens - CAP) // P) + 1):
                cost = used + CAP + (m - 1) * P + 1
                if cost <= choices and cost < new.get(blocks + m, choices + 1):
                    new[blocks + m] = cost
        best = new
    return max(best)


def perceiver_moe(nc, x, ctx_in, mask, w_q, w_k, w_v, w_o, gate_w, Wg, Wu, Wd, cWg, cWu, cWd, out):
    B, S, D = x.shape
    M = ctx_in.shape[1]
    E, _, FI = Wg.shape
    CI = cWg.shape[2]
    NC = D // P
    T = B * S // P
    BT = P // S
    HD = 32
    H = D // HD
    MC = BT * M // P
    TOPK = 4
    F2 = FI - P
    OVB = -(-(B * S - CAP) // P)
    REGION = CAP + OVB * P
    LISTW = -(-E * REGION // P)
    KMAX = most_blocks(E, B * S, TOPK * B * S)
    SPARE = 256
    STEP = P // 2
    ZEROED = SPARE // STEP * DMA
    ZEROED_XN = SPARE // P * DMA
    CAP2 = CAP - P
    XS_SCALE = float(D) ** -0.5
    SS_SCALE = float(HD) ** -0.5
    assert BT == 2 and T % 2 == 0 and H * S == 1024 and E * REGION == LISTW * P and CI == P and F2 == 64
    assert B * S % SPARE == 0 and CAP <= SPARE and ZEROED > 2 * DMA

    mask = mask.bitcast(U8)
    xf = x.rearrange("b s d -> (b s) d")
    cf = ctx_in.rearrange("b m d -> (b m) d")
    of = out.rearrange("b s d -> (b s) d")

    xn_dram = nc.dram_tensor("xn_scratch", (B * S + SPARE, D), F32, kind="Internal").ap()
    acc_dram = nc.dram_tensor("x2_scratch", (B * S + SPARE, D), F32, kind="Internal").ap()
    list_dram = nc.dram_tensor("list_scratch", (E * REGION, 2), I32, kind="Internal").ap()

    with ExitStack() as stack:
        def sb(name, shape, dt=F32):
            return stack.enter_context(nc.sbuf_tensor(name, shape, dt))

        def sem(name):
            return stack.enter_context(nc.semaphore(name))

        def flat(t):
            return t[:, :, :].rearrange("p a b -> p (a b)")

        tpair = stack.enter_context(nc.psum_tensor("tpair", [P, 2, 512], F32))
        bank2 = stack.enter_context(nc.psum_tensor("bank2", [P, 512], F32))
        pair = stack.enter_context(nc.psum_tensor("pair", [P, 2, 512], F32))
        bank5 = stack.enter_context(nc.psum_tensor("bank5", [P, 512], F32))
        bank6 = stack.enter_context(nc.psum_tensor("bank6", [P, 512], F32))
        bank7 = stack.enter_context(nc.psum_tensor("bank7", [P, 512], F32))
        tp = [tpair[:, 0, :], tpair[:, 1, :]]
        xb = bank2
        s2 = pair
        qo = bank5
        ko = bank6
        vl = bank7

        ident = sb("ident", [P, P])
        tri = sb("tri", [P, P], BF16)
        ones = sb("ones", [P, P], BF16)
        neghalf = sb("neghalf", [P, 1])
        iota_e = sb("iota_e", [P, E])
        base_e = sb("base_e", [P, E])

        wT = {n: sb(f"{n}T", [P, NC, D]) for n in ("wq", "wk", "wv", "wo")}
        gateT = sb("gateT", [P, NC, E])
        x_in = sb("x_in", [P, 2, D])
        ctx_sb = sb("ctx_sb", [P, 2, MC, D])
        mask_u8 = sb("mask_u8", [P, 2, M], U8)
        maskb = sb("maskb", [P, M])
        valid = sb("valid", [P, 1])
        ctxT_buf = sb("ctxT_buf", [P, NC * MC * P])
        ctxT = ctxT_buf[:, :].rearrange("p (c n) -> p c n", c=NC)
        stat = sb("stat", [P, 3, 6])
        mv = sb("mv", [P, 3, 2])
        vare = sb("vare", [P, 3])
        rstd = sb("rstd", [P, 3])
        xn1 = sb("xn1", [P, D])
        xn2 = sb("xn2", [P, D])
        xn3 = sb("xn3", [P, 2, D])
        xn1T = sb("xn1T", [P, NC, P])
        xn2T = sb("xn2T", [P, NC, P])
        xn3T = sb("xn3T", [P, NC, P])
        xsc = sb("xsc", [P, M])
        xmax = sb("xmax", [P, 1])
        xnb = sb("xnb", [P, 1])
        xsum = sb("xsum", [P, 1])
        xrs = sb("xrs", [P, 1])
        xrv = sb("xrv", [P, 1])
        xp = sb("xp", [P, M])
        xpT = sb("xpT", [P, M // P, P])
        x2 = sb("x2", [P, 2, D])
        qT = sb("qT", [P, NC, P])
        kT = sb("kT", [P, NC, P])
        v_sb = sb("v_sb", [P, D])
        smax = sb("smax", [P, H])
        ssum = sb("ssum", [P, H])
        srec = sb("srec", [P, H])
        probs_buf = sb("probs_buf", [P, 2 * H * S])
        sp_sb = probs_buf[:, 0:H * S].rearrange("p (h k) -> p h k", k=S)
        pT = probs_buf[:, H * S:].rearrange("p (j q) -> p j q", q=P)
        attnT = sb("attnT", [P, NC, P])
        logit = sb("logit", [P, E])
        floored = sb("floored", [P, E])
        lmax = sb("lmax", [P, 1])
        enl = sb("enl", [P, E])
        el = sb("el", [P, E])
        sg1 = sb("sg1", [P, E])
        score = sb("score", [P, E])
        top8 = sb("top8", [P, 8])
        idx8 = sb("idx8", [P, 8], U32)
        idxf = sb("idxf", [P, TOPK])
        hot = sb("hot", [P, TOPK, E])
        sel = sb("sel", [P, E], BF16)
        prod = sb("prod", [P, TOPK, E])
        prod2 = sb("prod2", [P, TOPK, E])
        wraw = sb("wraw", [P, TOPK])
        wsum = sb("wsum", [P, 1])
        wrec = sb("wrec", [P, 1])
        zrow = sb("zrow", [P, D])
        run = sb("run", [P, E])
        slotb = sb("slotb", [P, E])
        slotf = sb("slotf", [P, TOPK])
        slot = sb("slot", [P, 2, TOPK], I32)
        tokf = sb("tokf", [P, 1])
        entry = sb("entry", [P, 2, TOPK, 2], I32)
        names = ("ln1_var ln1_rstd ln1_done xs_done xmax_done xexp_done xrv_done pv_done x1_done "
                 "ln2_var ln2_rstd ln2_done q_done k_done v_done qT_done kT_done vsb_done ss0_done ss1_done "
                 "ssub0_done ssub1_done sexp0_done sexp1_done sp0_done sp1_done av_done attnT_done o_done x2_done ln3_var ln3_rstd ln3_done "
                 "logit_done lmax_done lexp_done sel_done rank_done slot_done").split()
        sig = {n: sem(n) for n in names}
        tp_full = [sem("tp_full0"), sem("tp_full1")]
        tp_copied = [sem("tp_copied0"), sem("tp_copied1")]
        const_ready = sem("const_ready")
        ident_ready = sem("ident_ready")
        w_loaded = {n: sem(f"{n}_loaded") for n in ("wq", "wk", "wv", "wo", "gate")}
        x_loaded = [sem("x_loaded0"), sem("x_loaded1")]
        ctx_loaded = [sem("ctx_loaded0"), sem("ctx_loaded1")]
        x2_stored = [sem("x2_stored0"), sem("x2_stored1")]
        xn_stored = [sem("xn_stored0"), sem("xn_stored1")]
        list_zeroed = sem("list_zeroed")
        scattered = sem("scattered")
        slots_used = sem("slots_used")
        dve_chain = sem("dve_chain")
        pool_chain = sem("pool_chain")
        settled = sem("settled")
        row_tile_done = sem("row_tile_done")
        lists_ready = sem("lists_ready")
        lists_empty = sem("lists_empty")

        probs_parts = [probs_buf[:, c * D:(c + 1) * D] for c in range(NC)]
        stage_w = {"wq": probs_parts, "wk": [x2[:, 0, :], x2[:, 1, :], xn3[:, 0, :], xn3[:, 1, :]],
                   "wv": [v_sb[:, :], flat(qT), flat(attnT), flat(kT)], "wo": probs_parts}
        stage_g = sb("stage_g", [E, D])
        meta = sb("meta", [P, E])

        raw_gu = [flat(wT[n])[:, 0:2 * NC * FI].rearrange("p (c i) -> p c i", c=NC) for n in ("wq", "wk")]
        raw_d = [flat(wT["wv"])[:, n * 2 * D:(n + 1) * 2 * D].rearrange("p (k d) -> p k d", k=2) for n in range(2)]
        raw_c = flat(wT["wo"])[:, 0:2 * NC * CI].rearrange("p (s c i) -> p s c i", s=2, c=NC)
        raw_cd = flat(wT["wo"])[:, 2 * NC * CI:2 * NC * CI + D]
        gu = [[sb(f"gu_{part}{n}", [P, NC, 2 * FI], F32R) for part in ("hi", "lo")] for n in range(2)]
        dn = [[sb(f"dn_{part}{n}", [P, 2, D], F32R) for part in ("hi", "lo")] for n in range(2)]
        cgu = [[sb(f"cgu_{part}{n}", [P, 2, NC, CI], F32R) for part in ("hi", "lo")] for n in range(2)]
        cdn = [[sb(f"cdn_{part}{n}", [P, D], F32R) for part in ("hi", "lo")] for n in range(2)]
        xT = [[sb(f"xT_{part}{n}", [P, NC, CAP], F32R) for part in ("hi", "lo")] for n in range(2)]
        aT = [[sb(f"aT_{part}{n}", [P, 3, 2 * P], F32R) for part in ("hi", "lo")] for n in range(2)]
        xg = [ctx_sb[:, n, 0:2, :] for n in range(2)]
        y_sb = [ctx_sb[:, n, 2:4, :] for n in range(2)]
        act_g = sp_sb[:, :, :].rearrange("p h k -> p (h k)")[:, 0:3 * CAP].rearrange("p (k n) -> p k n", k=3)
        act_a = probs_buf[:, H * S:H * S + 3 * CAP].rearrange("p (k n) -> p k n", k=3)
        idx = [sb(f"idx{n}", [P, 2, 2], I32) for n in range(4)]
        back = [sb(f"back{n}", [P, 2, 2], I32) for n in range(4)]
        g_bank = [xb, pair[:, 0, :], pair[:, 1, :]]
        y_bank = [qo, ko]
        names_b = ("xT_full xhi_done xlo_done whi_done wlo_done gu_done silu_done mul_done dhi_done dlo_done ahi_done "
                   "alo_done y0_full y1_full y0_done y1_done").split()
        sg = {n: sem(n) for n in names_b}
        gu_loaded = [sem("gu_loaded0"), sem("gu_loaded1")]
        d_loaded = [sem("d_loaded0"), sem("d_loaded1")]
        c_loaded = sem("c_loaded")
        cd_loaded = sem("cd_loaded")
        idx_loaded = [sem(f"idx_loaded{n}") for n in range(4)]
        gathered = [sem("gathered0"), sem("gathered1")]
        back_loaded = [sem(f"back_loaded{n}") for n in range(4)]
        added = sem("added")
        pads_zero = sem("pads_zero")

        meta_f = sb("meta_f", [1, 4, KMAX])
        meta_i = sb("meta_i", [1, 4, KMAX], I32)
        meta_half = sb("meta_half", [1, KMAX], I32)
        sc = ctxT_buf[:, 0:E * E].rearrange("p (a b) -> p a b", b=E)
        sc2 = ctxT_buf[:, E * E:2 * E * E].rearrange("p (a b) -> p a b", b=E)
        cnt = sb("cnt", [P, E])
        cnt_i = sb("cnt_i", [1, E], I32)
        counted = sem("counted")
        nblk = sb("nblk", [P, E])
        cum = sb("cum", [P, E])
        ordi = sb("ordi", [1, KMAX])
        lower = sb("lower", [P, E, E], BF16)
        thr = sb("thr", [P, OVB])
        idx_c = sb("idx_c", [P, 2], I32)
        meta_ready = sem("meta_ready")
        sc_names = "c_idx_loaded c_w_loaded c_gathered c_xT_full c_xT_done c_gu_done c_silu_done c_mul_done c_y_full c_y_done c_added".split()
        sv = {n: sem(n) for n in sc_names}

        y_complete = sem("y_complete")
        out_stored = sem("out_stored")
        empty = sb("empty", [P, LISTW, 2], I32)

        ORDER = {
            "cross": "ctx0 ctx1 ctx2 ctx3 xn1T wq0 wq1 wq2 wq3 wk0 wk1 xpT wk2 wk3 wv0 wv1 wv2 wv3 gate0 gate1 "
                     "wo0 wo1 wo2 wo3",
            "first": "ctx0 xn2T ctx1 ctx2 ctx3 xn1T pT0 pT1 xpT",
            "loop": "ctx0 xn2T ctx1 xn3T ctx2 ctx3 xn1T pT0 pT1 xpT",
            "last": "xn2T xn3T pT0 pT1",
            "tail": "xn3T",
        }
        ORDER = {mode: names.split() for mode, names in ORDER.items()}
        START = {"cross": 0}
        START["first"] = START["cross"] + len(ORDER["cross"])
        START["loop"] = START["first"] + len(ORDER["first"])
        START["last"] = START["loop"] + (T - 2) * len(ORDER["loop"])
        START["tail"] = START["last"] + len(ORDER["last"])
        assert len(ORDER["loop"]) % 2 == 0

        def fill_of(t, name, mode):
            k = START[mode] + ORDER[mode].index(name)
            before = (t - 1) * (len(ORDER["loop"]) // 2) if mode == "loop" else 0
            return k % 2, before + k // 2

        def wait_copied(eng, t, name, mode):
            b, m = fill_of(t, name, mode)
            eng.wait_ge(tp_copied[b], m + 1)

        block = stack.enter_context(nc.Block())

        class Tile:

            def __init__(self, i, m):
                self.i, self.m = i, m
                self.t = i * 2 + m
                self.par, self.half = m % 2, i + m // 2

            def ahead(self, k):
                return Tile(self.i, self.m + k)

        def tiles(eng, body):
            body(Tile(0, 0), "first")
            with eng.Fori(0, T // 2 - 1) as i:
                body(Tile(i, 1), "loop")
                body(Tile(i, 2), "loop")
            body(Tile(T // 2 - 1, 1), "last")

        class Expert:

            def __init__(self, i, m):
                self.i, self.m = i, m
                self.e = i * 4 + m
                self.par, self.pair_par = m % 2, m // 2 % 2
                self.half = i * 2 + m // 2
                self.first_of_pair = m % 2 == 0
                self.ring, self.round = m % 4, i + m // 4

            def ahead(self, k):
                other = Expert(self.i, self.m + k)
                return None if isinstance(other.e, int) and not 0 <= other.e < E else other

        def experts(eng, step):
            step(Expert(0, 0))
            with eng.Fori(0, E // 4 - 1) as i:
                for m in range(1, 5):
                    step(Expert(i, m))
            for m in range(1, 4):
                step(Expert(E // 4 - 1, m))

        def overflow(eng, step):
            eng.wait_ge(meta_ready, 1)
            count = eng.value_load(meta_i[0:1, 0, 0:1], min_val=0, max_val=KMAX)
            with eng.If(count > 0):
                with eng.Fori(0, count) as k:
                    step(k)

        def settle(eng):
            eng.sem_inc(settled, 1)

        def place(h):
            return (h % 2) * 8 + (h % 4) // 2 * 4 + h // 4

        def spread(ap, dim, n):
            shape = list(ap.shape)
            return ap.unsqueeze(dim).broadcast_to(shape[:dim] + [n] + shape[dim:])

        def chunks(ap, n):
            return ap.rearrange("p (c n) -> p c n", n=n)

        @block.sync
        def _(sp):
            for q in x2_stored + xn_stored:
                sp.sem_inc(q, CREDIT * DMA)

            def load_x(x):
                sp.dma_start(x_in[:, x.par, :], xf[bass.ds(x.t * P, P), :]).then_inc(x_loaded[x.par], DMA)

            def load_ctx(x):
                sp.dma_start(ctx_sb[:, x.par, :, :], cf[bass.ds(x.t * (MC * P), MC * P), :].rearrange(
                    "(c p) d -> p c d", p=P)).then_inc(ctx_loaded[x.par], DMA)
                for b in range(BT):
                    sp.dma_start(mask_u8[b * S:(b + 1) * S, x.par, :],
                                 mask[bass.ds(x.t * BT + b, 1), :].broadcast_to([S, M])).then_inc(
                                     ctx_loaded[x.par], DMA)

            def load_w(name, w):
                for c in range(NC):
                    sp.dma_start(stage_w[name][c], w[c * P:(c + 1) * P, :]).then_inc(w_loaded[name], DMA)

            load_x(Tile(0, 0))
            load_ctx(Tile(0, 0))
            load_w("wq", w_q)
            load_w("wk", w_k)
            load_w("wv", w_v)
            sp.dma_start(stage_g[:, :], gate_w).then_inc(w_loaded["gate"], DMA)
            load_x(Tile(0, 1))
            load_ctx(Tile(0, 1))
            b, m = fill_of(0, "wq3", "cross")
            sp.wait_ge(tp_full[b], m + 1)
            load_w("wo", w_o)
            sp.wait_ge(lists_empty, 1)
            sp.dma_start(list_dram.rearrange("(p n) o -> p (n o)", p=P),
                         empty[:, :, :].rearrange("p n two -> p (n two)")).then_inc(list_zeroed, DMA)

            def store_rows(x):
                sp.wait_ge(sig["x2_done"], x.t + 1 + CREDIT)
                sp.dma_start(acc_dram[bass.ds(x.t * P, P), :], x2[:, x.par, :]).then_inc(x2_stored[x.par], DMA)
                if not (isinstance(x.t, int) and x.t + 2 >= T):
                    load_x(x.ahead(2))
                sp.wait_ge(sig["ln3_done"], x.t + 1 + CREDIT)
                sp.dma_start(xn_dram[bass.ds(x.t * P, P), :], xn3[:, x.par, :]).then_inc(xn_stored[x.par], DMA)

            def body(x):
                if not isinstance(x.t, int) or x.t > 0:
                    store_rows(x.ahead(-1))
                if not (isinstance(x.t, int) and x.t + 2 >= T):
                    sp.wait_ge(sig["x1_done"], x.t + 1 + CREDIT)
                    load_ctx(x.ahead(2))

            body(Tile(0, 0))
            with sp.Fori(0, T // 2 - 2) as i:
                for m in (1, 2):
                    body(Tile(i, m))
            for m in (1, 2, 3):
                body(Tile(T // 2 - 2, m))
            store_rows(Tile(T // 2 - 1, 1))
            for q in x2_stored + xn_stored:
                sp.wait_ge(q, CREDIT * DMA + T // 2 * DMA)

            def load_gu(x, dst, q):
                for s, w in ((0, Wg), (1, Wu)):
                    sp.dma_start(dst[:, :, s * FI:(s + 1) * FI], w[bass.ds(x, 1)].rearrange("o (p c) i -> (o p) c i", c=NC)).then_inc(q, DMA)

            def load_d(x, dst, q):
                w = Wd[bass.ds(x, 1)].rearrange("o i d -> (o i) d")
                sp.dma_start(dst[:, 0, :], w[FI - P:FI, :]).then_inc(q, DMA)
                sp.dma_start(dst[P - F2:P, 1, :], w[0:F2, :]).then_inc(q, DMA)

            def load_c(x, q):
                for s, w in ((0, cWg), (1, cWu)):
                    sp.dma_start(raw_c[:, s, :, :], w[bass.ds(x, 1)].rearrange("o (p c) i -> (o p) c i", c=NC)).then_inc(q, DMA)

            def load_cd(x, q):
                sp.dma_start(raw_cd, cWd[bass.ds(x, 1)].rearrange("o i d -> (o i) d")).then_inc(q, DMA)

            def load_idx(x):
                sp.dma_start(idx[x.ring][:, :, :], list_dram[bass.ds(x.e * REGION, 2 * P), :].rearrange(
                    "(j p) o -> p j o", p=P), allow_slow_non_contiguous=True).then_inc(idx_loaded[x.ring], DMA)

            def load_back(x):
                sp.wait_ge(sg["y0_done"], x.e - 1 + CREDIT)
                sp.dma_start(back[x.ring][:, :, :], list_dram[bass.ds(x.e * REGION, 2 * P), :].rearrange(
                    "(j p) o -> p j o", p=P), allow_slow_non_contiguous=True).then_inc(back_loaded[x.ring], DMA)

            sp.wait_ge(sig["o_done"], T + CREDIT)
            load_gu(0, raw_gu[0], gu_loaded[0])
            load_c(0, c_loaded)
            sp.wait_ge(pads_zero, 1)
            load_d(0, raw_d[0], d_loaded[0])
            load_cd(0, cd_loaded)
            load_gu(1, raw_gu[1], gu_loaded[1])
            sp.wait_ge(lists_ready, 1)
            for m in range(3):
                load_idx(Expert(0, m))

            def step(x):
                nxt, nxt2, nxt3, last = x.ahead(1), x.ahead(2), x.ahead(3), x.ahead(-1)
                if nxt3 is not None:
                    sp.wait_ge(sg["xT_full"], x.e + CREDIT)
                    load_idx(nxt3)
                if nxt2 is not None:
                    sp.wait_ge(sg["wlo_done"], x.e + 1 + CREDIT)
                    load_gu(nxt2.e, raw_gu[x.par], gu_loaded[x.par])
                    if x.first_of_pair:
                        load_c(nxt2.half, c_loaded)
                if nxt is not None:
                    if last is not None:
                        sp.wait_ge(sg["dlo_done"], x.e + CREDIT)
                    load_d(nxt.e, raw_d[nxt.par], d_loaded[nxt.par])
                    if nxt.first_of_pair:
                        load_cd(nxt.half, cd_loaded)
                load_back(x)

            experts(sp, step)
            def block_c(k):
                sp.wait_ge(sv["c_added"], k + 1)
                settle(sp)
                ek = sp.value_load(meta_i[0:1, 1, bass.ds(k, 1)], min_val=0, max_val=E - 1)
                ck = sp.value_load(meta_i[0:1, 2, bass.ds(k, 1)], min_val=0, max_val=E // 2 - 1)
                rk = sp.value_load(meta_i[0:1, 3, bass.ds(k, 1)], min_val=0, max_val=E * REGION - P)
                sp.dma_start(idx_c[:, :], list_dram[bass.ds(rk, P), :]).then_inc(sv["c_idx_loaded"], DMA)
                sp.wait_ge(sg["wlo_done"], E - 1 + CREDIT)
                load_gu(ek, raw_gu[0], sv["c_w_loaded"])
                load_c(ck, sv["c_w_loaded"])
                sp.wait_ge(sg["dlo_done"], E - 1 + CREDIT)
                load_d(ek, raw_d[0], sv["c_w_loaded"])
                load_cd(ck, sv["c_w_loaded"])

            overflow(sp, block_c)
            sp.wait_ge(y_complete, 1)
            sp.dma_start(of, acc_dram[0:B * S, :]).then_inc(out_stored, DMA)
            sp.wait_ge(out_stored, DMA)

        @block.gpsimd
        def _(pool):
            def power(n, col, t):
                pool.wait_ge(sig[f"{n}_var"], t + 1 + CREDIT)
                nc.gpsimd.tensor_tensor(rstd[:, col:col + 1], vare[:, col:col + 1], neghalf[:, :],
                                        ALU.pow).then_inc(sig[f"{n}_rstd"], 1)

            for n in ("ln1_rstd", "ln2_rstd", "ln3_rstd"):
                pool.sem_inc(sig[n], CREDIT)
            pool.sem_inc(slots_used, CREDIT - 1)
            nc.gpsimd.memset(ident[:, :], 0.0).then_inc(pool_chain, 1)
            nc.gpsimd.memset(neghalf[:, :], -0.5).then_inc(pool_chain, 1)
            pool.wait_ge(pool_chain, 2)
            nc.gpsimd.affine_select(out=ident[:, :], in_=ident[:, :], compare_op=ALU.not_equal, fill=1.0, base=0,
                                    pattern=[[-1, P]], channel_multiplier=1).then_inc(ident_ready, 1)
            nc.gpsimd.memset(zrow[:, :], 0.0).then_inc(pool_chain, 1)
            nc.gpsimd.memset(empty[:, :, 1], 0).then_inc(pool_chain, 1)
            nc.gpsimd.iota(empty[:, :, 0], [[1, LISTW]], base=0, channel_multiplier=LISTW).then_inc(pool_chain, 1)
            nc.gpsimd.memset(tri[:, :], 0.0).then_inc(pool_chain, 1)
            nc.gpsimd.memset(ones[:, :], 1.0).then_inc(pool_chain, 1)
            nc.gpsimd.iota(iota_e[:, :], [[1, E]], base=0, channel_multiplier=0,
                           allow_small_or_imprecise_dtypes=True).then_inc(pool_chain, 1)
            nc.gpsimd.iota(base_e[:, :], [[REGION, E]], base=0, channel_multiplier=0,
                           allow_small_or_imprecise_dtypes=True).then_inc(pool_chain, 1)
            nc.gpsimd.iota(tokf[:, :], [[0, 1]], base=0, channel_multiplier=1,
                           allow_small_or_imprecise_dtypes=True).then_inc(pool_chain, 1)
            nc.gpsimd.iota(ordi[:, :], [[1, KMAX]], base=0, channel_multiplier=0,
                           allow_small_or_imprecise_dtypes=True).then_inc(pool_chain, 1)
            nc.gpsimd.iota(thr[:, :], [[P, OVB]], base=CAP, channel_multiplier=0,
                           allow_small_or_imprecise_dtypes=True).then_inc(pool_chain, 1)
            nc.gpsimd.memset(lower[:, :, :], 1.0).then_inc(pool_chain, 1)
            pool.wait_ge(pool_chain, 13)
            nc.gpsimd.affine_select(out=lower[:, :, :], in_=lower[:, :, :], compare_op=ALU.is_ge, fill=0.0, base=0,
                                    pattern=[[1, E], [-1, E]], channel_multiplier=0).then_inc(pool_chain, 1)
            nc.gpsimd.affine_select(out=tri[:, :], in_=tri[:, :], compare_op=ALU.is_ge, fill=1.0, base=0,
                                    pattern=[[-1, P]], channel_multiplier=1).then_inc(pool_chain, 1)
            pool.wait_ge(pool_chain, 15)
            pool.sem_inc(const_ready, 1)
            power("ln1", 0, 0)
            for n in range(B * S, B * S + SPARE, STEP):
                nc.gpsimd.dma_start(acc_dram[n:n + STEP, :], zrow[0:STEP, :]).then_inc(added, DMA)
            for n in range(B * S, B * S + SPARE, P):
                nc.gpsimd.dma_start(xn_dram[n:n + P, :], zrow[:, :]).then_inc(scattered, DMA)

            power("ln2", 1, 0)
            pool.wait_ge(list_zeroed, DMA)

            def scatter(x):
                pool.wait_ge(sig["slot_done"], x.t + 1 + CREDIT)
                pool.wait_ge(scattered, x.t * (TOPK * DMA) + ZEROED_XN)
                pool.sem_inc(slots_used, 1)
                settle(pool)
                for k in range(TOPK):
                    nc.gpsimd.indirect_dma_start(
                        list_dram, bass.IndirectOffsetOnAxis(ap=slot[:, x.par, k:k + 1], axis=0),
                        entry[:, x.par, k, :], None).then_inc(scattered, DMA)

            def body(x, mode):
                if mode != "first":
                    power("ln3", 2, x.t - 1)
                if mode != "last":
                    power("ln1", 0, x.t + 1)
                    power("ln2", 1, x.t + 1)
                if mode != "first":
                    scatter(x.ahead(-1))

            tiles(pool, body)
            power("ln3", 2, T - 1)
            scatter(Tile(T // 2 - 1, 1))
            pool.wait_ge(scattered, T * (TOPK * DMA) + ZEROED_XN)
            pool.sem_inc(lists_ready, 1)

            for q in xn_stored + x2_stored:
                pool.wait_ge(q, CREDIT * DMA + T // 2 * DMA)
            pool.wait_ge(added, ZEROED)

            def gather(dst, at):
                return nc.gpsimd.indirect_dma_start(dst, None, xn_dram, bass.IndirectOffsetOnAxis(ap=at, axis=0))

            def gather_rows(x):
                pool.wait_ge(idx_loaded[x.ring], (x.round + 1) * DMA)
                if not isinstance(x.e, int) or x.e >= 2:
                    pool.wait_ge(sg["xT_full"], x.e - 1 + CREDIT)
                settle(pool)
                gather(xg[x.par][:, 0, :], idx[x.ring][:, 0, 0:1]).then_inc(gathered[x.par], DMA)
                gather(xg[x.par][0:CAP2, 1, :], idx[x.ring][0:CAP2, 1, 0:1]).then_inc(gathered[x.par], DMA)

            def add(src, at):
                return nc.gpsimd.indirect_dma_start(acc_dram, bass.IndirectOffsetOnAxis(ap=at, axis=0), src, None,
                                                    compute_op=ALU.add)

            def add_rows(x):
                pool.wait_ge(back_loaded[x.ring], (x.round + 1) * DMA)
                pool.wait_ge(sg["y0_done"], x.e + 1 + CREDIT)
                pool.wait_ge(sg["y1_done"], x.e + 1 + CREDIT)
                pool.wait_ge(added, x.e * (2 * DMA) + ZEROED)
                settle(pool)
                add(y_sb[x.par][:, 0, :], back[x.ring][:, 0, 0:1]).then_inc(added, DMA)
                add(y_sb[x.par][0:CAP2, 1, :], back[x.ring][0:CAP2, 1, 0:1]).then_inc(added, DMA)

            gather_rows(Expert(0, 0))
            gather_rows(Expert(0, 1))
            gather_rows(Expert(0, 2))

            def step(x):
                if x.ahead(3) is not None:
                    gather_rows(x.ahead(3))
                else:
                    first_of_c(x)
                if x.ahead(-1) is not None:
                    add_rows(x.ahead(-1))


            def gather_c(k):
                pool.wait_ge(sv["c_idx_loaded"], (k + 1) * DMA)
                settle(pool)
                gather(xg[0][:, 0, :], idx_c[:, 0:1]).then_inc(sv["c_gathered"], DMA)

            def add_c(k):
                pool.wait_ge(sv["c_y_done"], k + 1)
                pool.wait_ge(added, k * DMA + ZEROED + E * 2 * DMA)
                settle(pool)
                add(y_sb[0][:, 0, :], idx_c[:, 0:1]).then_inc(added, DMA)
                pool.wait_ge(added, k * DMA + ZEROED + (E * 2 + 1) * DMA)
                pool.sem_inc(sv["c_added"], 1)

            def first_of_c(x):
                if x.par == 1:
                    return
                pool.wait_ge(sg["xT_full"], x.e + 1 + CREDIT)
                with pool.If(count > 0):
                    gather_c(0)

            pool.wait_ge(meta_ready, 1)
            count = pool.value_load(meta_i[0:1, 0, 0:1], min_val=0, max_val=KMAX)
            pool.sem_inc(sv["c_added"], 1)
            experts(pool, step)
            add_rows(Expert(E // 4 - 1, 3))
            with pool.If(count > 0):
                add_c(0)
            with pool.If(count > 1):
                with pool.Fori(1, count) as k:
                    gather_c(k)
                    add_c(k)
            pool.wait_ge(added, ZEROED + E * 2 * DMA)
            pool.sem_inc(y_complete, 1)

        @block.tensor
        def _(pe):
            for n in ("xs_done pv_done q_done k_done v_done ss0_done ss1_done av_done o_done logit_done rank_done").split():
                pe.sem_inc(sig[n], CREDIT)
            pe.wait_ge(ident_ready, 1)

            def fill(t, name, mode, parts, *after):
                b, m = fill_of(t, name, mode)
                if not (isinstance(m, int) and m == 0):
                    pe.wait_ge(tp_copied[b], m)
                for s, v in after:
                    pe.wait_ge(s, v)
                for dst, src, size in parts(tp[b]):
                    last = nc.tensor.transpose(dst, src, ident[0:size, 0:size])
                last.then_inc(tp_full[b], 1)

            def turn_w(name, *chunk):
                pe.wait_ge(w_loaded[name], NC * DMA)
                for dc in chunk:
                    fill(0, f"{name}{dc}", "cross", lambda b: [
                        (b[:, ec * P:(ec + 1) * P], stage_w[name][ec][:, dc * P:(dc + 1) * P], P) for ec in range(NC)])

            def turn_gate():
                pe.wait_ge(w_loaded["gate"], DMA)
                for half in range(2):
                    fill(0, f"gate{half}", "cross", lambda b: [
                        (b[:, j * E:(j + 1) * E], stage_g[:, (half * 2 + j) * P:(half * 2 + j + 1) * P], E)
                        for j in range(2)])

            def turn_ctx(t, y, mode, *chunk):
                for dc in chunk:
                    fill(t, f"ctx{dc}", mode, lambda b: [
                        (b[:, c * P:(c + 1) * P], ctx_sb[:, y.par, c, dc * P:(dc + 1) * P], P) for c in range(MC)])

            def turn(src, n=NC):
                return lambda b: [(b[:, c * P:(c + 1) * P], src[:, c * P:(c + 1) * P], P) for c in range(n)]

            def mm4(dst, lhsT, rhs):
                for c in range(NC):
                    last = nc.tensor.matmul(dst, lhsT[:, c, :], rhs[:, c, :], start=(c == 0), stop=(c == NC - 1))
                return last

            def ctx_here(y):
                pe.wait_ge(ctx_loaded[y.par], (y.half + 1) * ((1 + BT) * DMA))

            def cross_scores(t, y, mode):
                for name in ("ctx2", "ctx3", "xn1T"):
                    wait_copied(pe, t, name, mode)
                pe.wait_ge(sig["x1_done"], y.t + CREDIT)
                for c in range(NC):
                    for b in range(BT):
                        r = slice(b * S, (b + 1) * S)
                        last = nc.tensor.matmul(xb[r, 0:M], xn1T[:, c, r], ctxT[:, c, b * M:(b + 1) * M],
                                                start=(c == 0), stop=(c == NC - 1))
                last.then_inc(sig["xs_done"], 1)

            def readout(t, y, mode):
                wait_copied(pe, t, "xpT", mode)
                for c in range(M // P):
                    for b in range(BT):
                        r = slice(b * S, (b + 1) * S)
                        last = nc.tensor.matmul(xb[r, :], xpT[:, c, r], ctx_sb[:, y.par, b * (M // P) + c, :],
                                                start=(c == 0), stop=(c == M // P - 1))
                last.then_inc(sig["pv_done"], 1)

            def project(w, dst, done):
                for ec in range(NC):
                    for dc in range(NC):
                        last = nc.tensor.matmul(dst[:, ec * P:(ec + 1) * P], wT[w][:, dc, ec * P:(ec + 1) * P],
                                                xn2T[:, dc, :], start=(dc == 0), stop=(dc == NC - 1))
                last.then_inc(sig[done], 1)

            def self_scores(x):
                pe.wait_ge(sig["qT_done"], x.t + 1 + CREDIT)
                pe.wait_ge(sig["kT_done"], x.t + 1 + CREDIT)
                pe.wait_ge(sig["ssub0_done"], x.t + CREDIT)
                pe.wait_ge(sig["ssub1_done"], x.t + CREDIT)
                for g in range(4):
                    if g >= 2:
                        pe.wait_ge(row_tile_done, 2 * x.t + g - 1)
                    r = slice(HD * g, HD * g + HD)
                    for h in range(g, H, 4):
                        a, at = place(h) // 8, place(h) % 8
                        for b in range(BT):
                            c = slice(b * S, (b + 1) * S)
                            last = nc.tensor.matmul(s2[c, a, at * S:(at + 1) * S], qT[r, h // 4, c],
                                                    kT[r, h // 4, c], start=True, stop=True)
                    last.then_inc(row_tile_done if g < 2 else sig[f"ss{g - 2}_done"], 1)

            def values():
                for b in range(BT):
                    for dc in range(NC):
                        for hh in range(2):
                            w = wT["wv"][:, dc, :].rearrange("p (g two n) -> p two g n", two=2, n=P)[:, hh]
                            last = nc.tensor.matmul(vl[hh * S:(hh + 1) * S, b * 2 * P:(b + 1) * 2 * P],
                                                    xn2T[:, dc, b * S:(b + 1) * S], w,
                                                    start=(dc == 0), stop=(dc == NC - 1))
                last.then_inc(sig["v_done"], 1)

            def turn_probs(x, mode, j):
                fill(x.t, f"pT{j}", mode, lambda b: [
                    (b[:, c * P:(c + 1) * P], sp_sb[:, 8 * j + 2 * c:8 * j + 2 * c + 2, :], P) for c in range(4)],
                    (sig[f"sp{j}_done"], x.t + 1 + CREDIT))

            def attention(x, mode, odd):
                wait_copied(pe, x.t, f"pT{odd}", mode)
                settle(pe)
                for h in range(odd, H, 2):
                    hh, j = place(h) % 2, place(h) // 2
                    for b in range(BT):
                        col = b * 2 * P + (h // 8) * P + (h % 4) * HD
                        at = (h // 8) * P + b * S
                        last = nc.tensor.matmul(
                            (qo, ko)[hh][HD * (h % 4):HD * (h % 4) + HD, at:at + S],
                            v_sb[hh * S:(hh + 1) * S, col:col + HD],
                            pT[hh * S:(hh + 1) * S, j, b * S:(b + 1) * S], start=True, stop=True)
                return last

            def logits(t, y, mode):
                wait_copied(pe, t, "xn3T", mode)
                pe.wait_ge(sig["slot_done"], y.t + CREDIT)
                mm4(vl[:, 0:E], xn3T, gateT).then_inc(sig["logit_done"], 1)

            def ranks(y):
                pe.wait_ge(const_ready, 1)
                pe.wait_ge(sig["sel_done"], y.t + 1 + CREDIT)
                nc.tensor.matmul(vl[:, E:2 * E], tri[:, :], sel[:, :], start=True, stop=True)
                nc.tensor.matmul(vl[:, 2 * E:3 * E], ones[:, :], sel[:, :], start=True,
                                 stop=True).then_inc(sig["rank_done"], 1)

            zero = Tile(0, 0)
            ctx_here(zero)
            turn_ctx(0, zero, "cross", 0, 1, 2, 3)
            fill(0, "xn1T", "cross", turn(xn1), (sig["ln1_done"], 1 + CREDIT))
            cross_scores(0, zero, "cross")
            turn_w("wq", 0, 1, 2, 3)
            turn_w("wk", 0, 1)
            fill(0, "xpT", "cross", turn(xp, M // P), (sig["xexp_done"], 1 + CREDIT))
            turn_w("wk", 2, 3)
            readout(0, zero, "cross")
            turn_w("wv", 0, 1, 2, 3)
            turn_gate()
            turn_w("wo", 0, 1, 2, 3)

            def step(x, mode):
                t, y, z = x.t, x.ahead(1), x.ahead(-1)
                if mode != "last":
                    ctx_here(y)
                    turn_ctx(t, y, mode, 0)
                fill(t, "xn2T", mode, turn(xn2), (sig["ln2_done"], t + 1 + CREDIT))
                if mode != "last":
                    turn_ctx(t, y, mode, 1)
                wait_copied(pe, t, "xn2T", mode)
                pe.wait_ge(sig["attnT_done"], t + CREDIT)
                project("wq", qo, "q_done")
                if mode != "first":
                    fill(t, "xn3T", mode, turn(xn3[:, z.par, :]), (sig["ln3_done"], t + CREDIT))
                if mode != "last":
                    turn_ctx(t, y, mode, 2)
                pe.wait_ge(sig["x2_done"], t + CREDIT)
                project("wk", ko, "k_done")
                if mode != "last":
                    turn_ctx(t, y, mode, 3)
                if mode != "first":
                    logits(t, z, mode)
                if mode != "last":
                    fill(t, "xn1T", mode, turn(xn1), (sig["ln1_done"], y.t + 1 + CREDIT))
                self_scores(x)
                pe.wait_ge(sig["lmax_done"], t + CREDIT)
                values()
                if mode != "last":
                    cross_scores(t, y, mode)
                turn_probs(x, mode, 0)
                turn_probs(x, mode, 1)
                pe.wait_ge(sig["vsb_done"], t + 1 + CREDIT)
                attention(x, mode, 0)
                if mode != "last":
                    fill(t, "xpT", mode, turn(xp, M // P), (sig["xexp_done"], y.t + 1 + CREDIT))
                attention(x, mode, 1).then_inc(sig["av_done"], 1)
                if mode != "first":
                    ranks(z)
                if mode != "last":
                    readout(t, y, mode)
                pe.wait_ge(sig["attnT_done"], t + 1 + CREDIT)
                mm4(ko[:, :], attnT, wT["wo"]).then_inc(sig["o_done"], 1)

            tiles(pe, step)
            end = Tile(T // 2 - 1, 1)
            fill(T - 1, "xn3T", "tail", turn(xn3[:, end.par, :]), (sig["ln3_done"], T + CREDIT))
            logits(T - 1, end, "tail")
            ranks(end)

            for n, c in (("xT_full", 1), ("gu_done", 3), ("y0_full", 1), ("y1_full", 1)):
                pe.sem_inc(sg[n], c * CREDIT)

            def turn_rows(x):
                pe.wait_ge(gathered[x.par], (x.half + 1) * (2 * DMA))
                pe.wait_ge(sg["xlo_done"], x.e + CREDIT)
                for c in range(NC):
                    o = (c % 2) * CAP
                    nc.tensor.transpose(tp[c // 2][:, o:o + P], xg[x.par][:, 0, c::NC], ident[:, :])
                    last = nc.tensor.transpose(tp[c // 2][:, o + P:o + CAP], xg[x.par][0:CAP2, 1, c::NC],
                                               ident[0:CAP2, 0:CAP2])
                last.then_inc(sg["xT_full"], 1)

            PARTS = ((0, 0), (1, 0), (0, 1))

            def more_than_128(x):
                return pe.value_load(cnt_i[0:1, bass.ds(x.e, 1)], min_val=0, max_val=B * S) > P

            def gate_up(x):
                pe.wait_ge(sg["xlo_done"], x.e + 1 + CREDIT)
                pe.wait_ge(sg["wlo_done"], x.e + 1 + CREDIT)
                w, cw, xs = gu[x.par], cgu[x.pair_par], xT[x.par]
                parts = [[lambda p, c, s=s: w[p][:, c, s * P:(s + 1) * P] for s in range(2)],
                         [lambda p, c: w[p][:, c, 2 * P:3 * P]],
                         [lambda p, c, s=s: cw[p][:, s, c, :] for s in range(2)]]
                for j, group in enumerate(parts):
                    pe.wait_ge(sg["mul_done"], x.e * 3 + (j + 1 + 3 * CREDIT - 3))
                    for s, lhsT in enumerate(group):
                        dst = g_bank[j][:, s * CAP:(s + 1) * CAP]
                        for c in range(NC):
                            for n, (pw, px) in enumerate(PARTS):
                                last = nc.tensor.matmul(dst, lhsT(pw, c), xs[px][:, c, :],
                                                        start=(c == 0 and n == 0), stop=(c == NC - 1 and n == 2))
                    last.then_inc(sg["gu_done"], 1)

            def down(x):
                pe.wait_ge(sg["alo_done"], x.e + 1 + CREDIT)
                pe.wait_ge(sg["dlo_done"], x.e + 1 + CREDIT)
                down_block(x, 0).then_inc(sg["y0_full"], 1)
                with pe.If(more_than_128(x)):
                    down_block(x, 1).then_inc(sg["y1_full"], 1)
                with pe.Else():
                    pe.wait_ge(sg["y1_done"], x.e + CREDIT)
                    pe.sem_inc(sg["y1_full"], 1)

            def down_block(x, blk):
                a, w, cw = aT[x.par], dn[x.par], cdn[x.pair_par]
                pe.wait_ge(sg[f"y{blk}_done"], x.e + CREDIT)
                tokens, half = slice(blk * P, (blk + 1) * P), slice(F2, P)
                terms = [(a[pa][:, 0, tokens], w[pw][:, 0, :]) for pa, pw in PARTS]
                terms += [(a[0][:, 1, tokens], w[0][:, 1, :]), (a[0][half, 1, tokens], w[1][half, 1, :])]
                terms += [(a[pa][:, 2, tokens], cw[pw][:, :]) for pa, pw in PARTS]
                for n, (lhsT, rhs) in enumerate(terms):
                    last = nc.tensor.matmul(y_bank[blk][:, :], lhsT, rhs, start=(n == 0), stop=(n == len(terms) - 1))
                return last

            pe.wait_ge(counted, 1)
            turn_rows(Expert(0, 0))

            def step(x):
                if x.ahead(1) is not None:
                    turn_rows(x.ahead(1))
                gate_up(x)
                if x.ahead(-1) is not None:
                    down(x.ahead(-1))

            experts(pe, step)
            down(Expert(E // 4 - 1, 3))

            def block_c(k):
                pe.wait_ge(sv["c_gathered"], (k + 1) * DMA)
                for c in range(NC):
                    last = nc.tensor.transpose(tp[0][:, c * P:(c + 1) * P], xg[0][:, 0, c::NC], ident[:, :])
                last.then_inc(sv["c_xT_full"], 1)
                pe.wait_ge(sv["c_xT_done"], k + 1)
                pe.wait_ge(sv["c_w_loaded"], (k + 1) * (7 * DMA))
                for j in range(3):
                    for s in range(1 if j == 1 else 2):
                        for c in range(NC):
                            o = 2 * P if j else s * P
                            lhsT = raw_gu[0][:, c, o:o + P] if j < 2 else raw_c[:, s, c, :]
                            last = nc.tensor.matmul(g_bank[j][:, s * P:(s + 1) * P], lhsT, xn1T[:, c, :],
                                                    start=(c == 0), stop=(c == NC - 1))
                last.then_inc(sv["c_gu_done"], 1)
                pe.wait_ge(sv["c_mul_done"], k + 1)
                for j in range(3):
                    rhs = raw_d[0][:, j, :] if j < 2 else raw_cd
                    last = nc.tensor.matmul(y_bank[0][:, :], act_a[:, j, 0:P], rhs, start=(j == 0), stop=(j == 2))
                last.then_inc(sv["c_y_full"], 1)

            overflow(pe, block_c)

        @block.scalar
        def _(act):
            for n in "xexp_done qT_done vsb_done sexp0_done sexp1_done lexp_done".split():
                act.sem_inc(sig[n], CREDIT)
            copy = nc.scalar.copy

            def cp(t, name, mode, dst, *after, n=NC):
                b, m = fill_of(t, name, mode)
                act.wait_ge(tp_full[b], m + 1)
                for s, v in after:
                    act.wait_ge(s, v)
                copy(dst, chunks(tp[b], P)[:, 0:n, :]).then_inc(tp_copied[b], 1)

            def cp_ctx(t, y, mode, dc):
                cp(t, f"ctx{dc}", mode, chunks(ctxT[:, dc, :], P), (sig["xs_done"], y.t + CREDIT))

            def cp_xn1(t, y, mode):
                cp(t, "xn1T", mode, xn1T[:, :, :], (sig["xs_done"], y.t + CREDIT))

            def cp_w(name, *chunk):
                for dc in chunk:
                    cp(0, f"{name}{dc}", "cross", chunks(wT[name][:, dc, :], P))

            def cross_exp(tt):
                act.wait_ge(sig["xmax_done"], tt + 1 + CREDIT)
                act.wait_ge(sig["xrv_done"], tt + CREDIT)
                nc.scalar.activation(xp[:, :], xsc[:, :], ACT.Exp, bias=xnb[:, :], scale=XS_SCALE,
                                     accum_out=xsum[:, :]).then_inc(sig["xexp_done"], 1)

            zero = Tile(0, 0)
            cp_ctx(0, zero, "cross", 0)
            cp_ctx(0, zero, "cross", 2)
            cp_xn1(0, zero, "cross")
            cp_w("wq", 0, 1)
            cross_exp(0)
            cp(0, "xpT", "cross", xpT[:, :, :], (sig["pv_done"], CREDIT), n=M // P)
            cp_w("wk", 3)
            cp_w("wv", 0, 1, 2, 3)
            for half in range(2):
                b, m = fill_of(0, f"gate{half}", "cross")
                act.wait_ge(tp_full[b], m + 1)
                copy(gateT[:, 2 * half:2 * half + 2, :], chunks(tp[b][:, 0:2 * E], E)).then_inc(tp_copied[b], 1)
            cp_w("wo", 0, 2)

            def gate_exp(z):
                act.wait_ge(sig["lmax_done"], z.t + 1 + CREDIT)
                nc.scalar.activation(enl[:, :], floored[:, :], ACT.Exp, scale=-1.0)
                nc.scalar.activation(el[:, :], logit[:, :], ACT.Exp, bias=lmax[:, :]).then_inc(sig["lexp_done"], 1)

            def body(x, mode):
                t, y, z = x.t, x.ahead(1), x.ahead(-1)
                cp(t, "xn2T", mode, xn2T[:, :, :], (sig["v_done"], t + CREDIT))
                if mode != "last":
                    cp_ctx(t, y, mode, 1)
                act.wait_ge(sig["q_done"], t + 1 + CREDIT)
                act.wait_ge(sig["ss1_done"], t + CREDIT)
                copy(qT[:, :, :], chunks(qo[:, :], P)).then_inc(sig["qT_done"], 1)
                if mode != "first":
                    cp(t, "xn3T", mode, xn3T[:, :, :], (sig["logit_done"], t - 1 + CREDIT))
                if mode != "last":
                    cp_ctx(t, y, mode, 2)
                    cp_ctx(t, y, mode, 3)
                if mode != "last":
                    cp_xn1(t, y, mode)
                if mode != "first":
                    gate_exp(z)
                for a in range(2):
                    act.wait_ge(sig[f"ssub{a}_done"], t + 1 + CREDIT)
                    nc.scalar.activation(sp_sb[:, 8 * a:8 * a + 8, :], sp_sb[:, 8 * a:8 * a + 8, :], ACT.Exp,
                                         scale=SS_SCALE).then_inc(sig[f"sexp{a}_done"], 1)
                act.wait_ge(sig["v_done"], t + 1 + CREDIT)
                act.wait_ge(sig["av_done"], t + CREDIT)
                copy(v_sb[:, :], vl[:, :]).then_inc(sig["vsb_done"], 1)
                cp(t, "pT0", mode, pT[:, 0:4, :], (sig["av_done"], t + CREDIT))
                if mode != "last":
                    cross_exp(y.t)
                    cp(t, "xpT", mode, xpT[:, :, :], (sig["pv_done"], y.t + CREDIT), n=M // P)

            tiles(act, body)
            cp(T - 1, "xn3T", "tail", xn3T[:, :, :], (sig["logit_done"], T - 1 + CREDIT))
            gate_exp(Tile(T // 2 - 1, 1))

            for n, c in (("xhi_done", 1), ("whi_done", 1), ("silu_done", 2), ("dhi_done", 1), ("ahi_done", 1),
                         ("y0_done", 1)):
                act.sem_inc(sg[n], c * CREDIT)

            def rows_hi(x):
                act.wait_ge(sg["xT_full"], x.e + 1 + CREDIT)
                act.wait_ge(sg["gu_done"], (x.e - 1 + CREDIT) * 3)
                copy(xT[x.par][0][:, :, :].rearrange("p (a c) n -> p a (c n)", a=2),
                     tpair[:, :, 0:2 * CAP]).then_inc(sg["xhi_done"], 1)

            def gu_hi(x):
                act.wait_ge(gu_loaded[x.par], (x.half + 1) * (2 * DMA))
                last = copy(gu[x.par][0][:, :, :], raw_gu[x.par])
                if x.first_of_pair:
                    act.wait_ge(c_loaded, (x.half + 1) * (2 * DMA))
                    last = copy(cgu[x.pair_par][0][:, :, :, :], raw_c)
                last.then_inc(sg["whi_done"], 1)

            def silu_large(n):
                nc.scalar.activation(act_g[F2:P, 1, 0:n], g_bank[0][0:F2, 0:n], ACT.Silu)
                nc.scalar.activation(act_g[0:F2, 0, 0:n], g_bank[0][F2:P, 0:n], ACT.Silu)
                return nc.scalar.activation(act_g[F2:P, 0, 0:n], g_bank[0][0:F2, n:2 * n], ACT.Silu)

            def silu(x):
                act.wait_ge(sg["gu_done"], (x.e + CREDIT) * 3 + 1)
                act.wait_ge(sg["mul_done"], (x.e + CREDIT) * 3)
                silu_large(CAP).then_inc(sg["silu_done"], 1)
                act.wait_ge(sg["gu_done"], (x.e + CREDIT) * 3 + 3)
                nc.scalar.activation(act_g[:, 2, :], g_bank[2][:, 0:CAP], ACT.Silu).then_inc(sg["silu_done"], 1)

            def d_hi(x):
                act.wait_ge(d_loaded[x.par], (x.half + 1) * (2 * DMA))
                act.wait_ge(sg["y0_full"], x.e - 1 + CREDIT)
                act.wait_ge(sg["y1_full"], x.e - 1 + CREDIT)
                copy(dn[x.par][0][:, 0, :], raw_d[x.par][:, 0, :])
                copy(dn[x.par][0][F2:P, 1, :], raw_d[x.par][F2:P, 1, :])
                last = copy(dn[x.par][0][0:F2, 1, :], raw_d[x.par][F2:P, 1, :])
                if x.first_of_pair:
                    act.wait_ge(cd_loaded, (x.half + 1) * DMA)
                    last = copy(cdn[x.pair_par][0][:, :], raw_cd)
                last.then_inc(sg["dhi_done"], 1)

            def a_hi(x):
                act.wait_ge(sg["mul_done"], (x.e + CREDIT) * 3 + 3)
                copy(aT[x.par][0][:, :, 0:CAP], act_a).then_inc(sg["ahi_done"], 1)

            def y_out(x):
                act.wait_ge(sg["y0_full"], x.e + 1 + CREDIT)
                act.wait_ge(added, x.e * (2 * DMA) + (ZEROED - 2 * DMA))
                act.wait_ge(back_loaded[x.ring], (x.round + 1) * DMA)
                nc.scalar.mul(y_sb[x.par][:, 0, :], y_bank[0][:, :], back[x.ring][:, 0, 1:2].bitcast(F32)).then_inc(
                    sg["y0_done"], 1)

            gu_hi(Expert(0, 0))
            rows_hi(Expert(0, 0))

            def step(x):
                if x.ahead(1) is not None:
                    rows_hi(x.ahead(1))
                    gu_hi(x.ahead(1))
                silu(x)
                d_hi(x)
                a_hi(x)
                if x.ahead(-1) is not None:
                    y_out(x.ahead(-1))

            act.wait_ge(pads_zero, 1)
            experts(act, step)
            y_out(Expert(E // 4 - 1, 3))

            def block_c(k):
                act.wait_ge(sv["c_gu_done"], k + 1)
                silu_large(P)
                nc.scalar.activation(act_g[:, 2, 0:P], g_bank[2][:, 0:P], ACT.Silu).then_inc(sv["c_silu_done"], 1)

            overflow(act, block_c)

        @block.vector
        def _(dve):
            v = nc.vector
            for n in ("ln1_var ln1_done xmax_done xrv_done x1_done ln2_var ln2_done kT_done ssub0_done ssub1_done sp0_done sp1_done "
                      "attnT_done x2_done ln3_var ln3_done lmax_done sel_done slot_done").split():
                dve.sem_inc(sig[n], CREDIT)

            class Chain:
                base, k = 0, 0

                def __call__(self, instruction):
                    self.k += 1
                    instruction.then_inc(dve_chain, 1)
                    dve.wait_ge(dve_chain, self.base + self.k)

            link = Chain()
            def norm_stats(col, src, n):
                link(v.bn_stats(stat[:, col, :], src))
                settle(dve)
                link(v.bn_aggr(mv[:, col, :], stat[:, col, :]))
                v.tensor_scalar_add(vare[:, col:col + 1], mv[:, col, 1:2], EPS).then_inc(sig[f"{n}_var"], 1)

            def norm_apply(col, src, dst, n, t):
                dve.wait_ge(sig[f"{n}_rstd"], t + 1 + CREDIT)
                v.tensor_scalar(dst, src, mv[:, col, 0:1], rstd[:, col:col + 1], ALU.subtract,
                                ALU.mult).then_inc(sig[f"{n}_done"], 1)

            def cp(t, name, mode, dst, *after):
                b, m = fill_of(t, name, mode)
                dve.wait_ge(tp_full[b], m + 1)
                for s, val in after:
                    dve.wait_ge(s, val)
                v.tensor_copy(dst, chunks(tp[b], P)).then_inc(tp_copied[b], 1)

            def cp_ctx(t, y, mode, dc):
                cp(t, f"ctx{dc}", mode, chunks(ctxT[:, dc, :], P), (sig["xs_done"], y.t + CREDIT))

            def cp_w(name, *chunk):
                for dc in chunk:
                    cp(0, f"{name}{dc}", "cross", chunks(wT[name][:, dc, :], P))

            def first_norm(y):
                dve.wait_ge(x_loaded[y.par], (y.half + 1) * DMA)
                norm_stats(0, x_in[:, y.par, :], "ln1")
                read_mask(y)
                norm_apply(0, x_in[:, y.par, :], xn1[:, :], "ln1", y.t)

            def read_mask(y):
                dve.wait_ge(ctx_loaded[y.par], (y.half + 1) * ((1 + BT) * DMA))
                link(v.tensor_scalar(maskb[:, :], mask_u8[:, y.par, :], 1.0, NEG, ALU.subtract, ALU.mult))
                link(v.tensor_reduce(valid[:, :], mask_u8[:, y.par, :], AX.X, ALU.max))

            def cross_max(tt):
                dve.wait_ge(sig["xs_done"], tt + 1 + CREDIT)
                dve.wait_ge(sig["xexp_done"], tt + CREDIT)
                settle(dve)
                link(v.tensor_tensor_reduce(out=xsc[:, :], in0=xb[:, 0:M], in1=maskb[:, :], scale=1.0,
                                            scalar=-3.0e38, op0=ALU.add, op1=ALU.max, accum_out=xmax[:, :]))
                v.tensor_scalar(xnb[:, :], xmax[:, :], -0.1 * NEG, -XS_SCALE, ALU.max, ALU.mult).then_inc(sig["xmax_done"], 1)

            def cross_sum(tt):
                dve.wait_ge(sig["xexp_done"], tt + 1 + CREDIT)
                link(v.tensor_scalar(xsum[:, :], xsum[:, :], 0.5, None, ALU.max))
                link(v.reciprocal(xrs[:, :], xsum[:, :]))
                v.tensor_tensor(xrv[:, :], xrs[:, :], valid[:, :], ALU.mult).then_inc(sig["xrv_done"], 1)

            def residual1(y):
                dve.wait_ge(sig["pv_done"], y.t + 1 + CREDIT)
                dve.wait_ge(sig["xrv_done"], y.t + 1 + CREDIT)
                x1 = x_in[:, y.par, :]
                v.scalar_tensor_tensor(out=x1, in0=xb[:, :], scalar=xrv[:, :], in1=x1,
                                       op0=ALU.mult, op1=ALU.add).then_inc(sig["x1_done"], 1)
                dve.wait_ge(sig["x1_done"], y.t + 1 + CREDIT)
                norm_stats(1, x1, "ln2")
                norm_apply(1, x1, xn2[:, :], "ln2", y.t)

            zero = Tile(0, 0)
            dve.wait_ge(x_loaded[0], DMA)
            norm_stats(0, x_in[:, 0, :], "ln1")
            norm_apply(0, x_in[:, 0, :], xn1[:, :], "ln1", 0)
            cp_ctx(0, zero, "cross", 1)
            cp_ctx(0, zero, "cross", 3)
            read_mask(zero)
            cross_max(0)
            cp_w("wq", 2, 3)
            cp_w("wk", 0, 1)
            cross_sum(0)
            cp_w("wk", 2)
            residual1(zero)
            dve.wait_ge(const_ready, 1)
            link(v.tensor_copy(run[:, :], base_e[:, :]))
            link(v.tensor_scalar(empty[:, :, 0], empty[:, :, 0], SPARE - 1, B * S, ALU.bitwise_and, ALU.bitwise_or))
            dve.sem_inc(lists_empty, 1)
            cp_w("wo", 1, 3)

            def residual2(z):
                dve.wait_ge(sig["o_done"], z.t + 1 + CREDIT)
                dve.wait_ge(x2_stored[z.par], (z.half + CREDIT) * DMA)
                v.tensor_tensor(x2[:, z.par, :], ko[:, :], x_in[:, z.par, :], ALU.add).then_inc(sig["x2_done"], 1)
                dve.wait_ge(sig["x2_done"], z.t + 1 + CREDIT)
                norm_stats(2, x2[:, z.par, :], "ln3")

            def third_norm(z):
                dve.wait_ge(xn_stored[z.par], (z.half + CREDIT) * DMA)
                norm_apply(2, x2[:, z.par, :], xn3[:, z.par, :], "ln3", z.t)

            def gate_max(z):
                dve.wait_ge(sig["logit_done"], z.t + 1 + CREDIT)
                v.tensor_scalar(floored[:, :], vl[:, 0:E], LOWEST, None, ALU.max)
                link(v.tensor_copy(logit[:, :], vl[:, 0:E]))
                v.tensor_reduce(lmax[:, :], logit[:, :], AX.X, ALU.max, negate=True).then_inc(sig["lmax_done"], 1)

            def choose(z):
                dve.wait_ge(sig["lexp_done"], z.t + 1 + CREDIT)
                link(v.tensor_scalar_add(sg1[:, :], enl[:, :], 1.0))
                link(v.reciprocal(score[:, :], sg1[:, :]))
                settle(dve)
                link(v.max(top8[:, :], score[:, :]))
                settle(dve)
                link(v.max_index(idx8[:, :], top8[:, :], score[:, :]))
                link(v.tensor_copy(idxf[:, :], idx8[:, 0:TOPK]))
                link(v.tensor_tensor(hot[:, :, :], spread(iota_e[:, :], 1, TOPK), spread(idxf[:, :], 2, E),
                                     ALU.is_equal))
                with nc.allow_low_precision(reason="zeros and ones"):
                    v.tensor_reduce(sel[:, :], hot[:, :, :].rearrange("p k e -> p e k"), AX.X, ALU.add).then_inc(
                        sig["sel_done"], 1)

            def weigh(z):
                t = z.t
                link(v.tensor_tensor(prod[:, :, :], hot[:, :, :], spread(el[:, :], 1, TOPK), ALU.mult))
                link(v.tensor_reduce(wraw[:, :], prod[:, :, :], AX.X, ALU.add))
                link(v.tensor_reduce(wsum[:, :], wraw[:, :], AX.X, ALU.add))
                link(v.reciprocal(wrec[:, :], wsum[:, :]))
                dve.wait_ge(slots_used, t - 1 + CREDIT)
                v.tensor_scalar(entry[:, z.par, :, 1].bitcast(F32), wraw[:, :], wrec[:, :], None, ALU.mult)
                v.tensor_copy(entry[:, z.par, :, 0], tokf[:, :].broadcast_to([P, TOPK]))

            def rows_of_lists(z):
                t = z.t
                dve.wait_ge(sig["rank_done"], t + 1 + CREDIT)
                link(v.tensor_tensor(slotb[:, :], vl[:, E:2 * E], run[:, :], ALU.add))
                link(v.tensor_tensor(prod2[:, :, :], hot[:, :, :], spread(slotb[:, :], 1, TOPK), ALU.mult))
                link(v.tensor_reduce(slotf[:, :], prod2[:, :, :], AX.X, ALU.add))
                link(v.tensor_scalar_add(tokf[:, :], tokf[:, :], float(P)))
                link(v.tensor_tensor(run[:, :], vl[:, 2 * E:3 * E], run[:, :], ALU.add))
                v.tensor_copy(slot[:, z.par, :], slotf[:, :]).then_inc(sig["slot_done"], 1)
                dve.wait_ge(sig["slot_done"], t + 1 + CREDIT)

            def step(x, mode):
                t, y, z = x.t, x.ahead(1), x.ahead(-1)
                if mode != "last":
                    cp_ctx(t, y, mode, 0)
                if mode != "first":
                    residual2(z)
                    third_norm(z)
                if mode != "last":
                    first_norm(y)
                dve.wait_ge(sig["k_done"], t + 1 + CREDIT)
                dve.wait_ge(sig["ss1_done"], t + CREDIT)
                v.tensor_copy(kT[:, :, :], chunks(ko[:, :], P)).then_inc(sig["kT_done"], 1)
                if mode != "first":
                    gate_max(z)
                for a in range(2):
                    half = slice(8 * a, 8 * a + 8)
                    dve.wait_ge(sig[f"ss{a}_done"], t + 1 + CREDIT)
                    scores = chunks(s2[:, a, :], S)
                    link(v.tensor_reduce(smax[:, half], scores, AX.X, ALU.max))
                    v.tensor_tensor(sp_sb[:, half, :], scores, spread(smax[:, half], 2, S),
                                    ALU.subtract).then_inc(sig[f"ssub{a}_done"], 1)
                for a in range(2):
                    half = slice(8 * a, 8 * a + 8)
                    dve.wait_ge(sig[f"sexp{a}_done"], t + 1 + CREDIT)
                    link(v.tensor_reduce(ssum[:, half], sp_sb[:, half, :], AX.X, ALU.add))
                    link(v.reciprocal(srec[:, half], ssum[:, half]))
                    v.tensor_tensor(sp_sb[:, half, :], sp_sb[:, half, :], spread(srec[:, half], 2, S),
                                    ALU.mult).then_inc(sig[f"sp{a}_done"], 1)
                if mode != "first":
                    choose(z)
                if mode != "last":
                    cross_max(y.t)
                cp(t, "pT1", mode, pT[:, 4:8, :], (sig["av_done"], t + CREDIT))
                if mode != "first":
                    weigh(z)
                if mode != "last":
                    cross_sum(y.t)
                dve.wait_ge(sig["av_done"], t + 1 + CREDIT)
                dve.wait_ge(sig["o_done"], t + CREDIT)
                for half_of, src in ((0, qo), (1, ko)):
                    last = v.tensor_copy(attnT[:, :, :].rearrange("p (c two) q -> p two c q", two=2)[:, half_of],
                                         chunks(src[:, 0:2 * P], P))
                last.then_inc(sig["attnT_done"], 1)
                if mode != "first":
                    rows_of_lists(z)
                if mode != "last":
                    residual1(y)

            step(zero, "first")
            first = link.k
            with dve.Fori(0, T // 2 - 1) as i:
                link.base, link.k = i * (2 * LINKS) + first, 0
                step(Tile(i, 1), "loop")
                assert link.k == LINKS, link.k
                step(Tile(i, 2), "loop")
            link.base, link.k = first + LINKS * (T - 2), 0
            step(Tile(T // 2 - 1, 1), "last")
            end = Tile(T // 2 - 1, 1)
            residual2(end)
            third_norm(end)
            gate_max(end)
            choose(end)
            weigh(end)
            rows_of_lists(end)
            link.base, link.k = link.base + link.k, 0

            for n, c in (("xlo_done", 1), ("wlo_done", 1), ("mul_done", 3), ("dlo_done", 1), ("alo_done", 1),
                         ("y1_done", 1)):
                dve.sem_inc(sg[n], c * CREDIT)
            dve.wait_ge(sig["o_done"], T + CREDIT)
            for n in range(2):
                v.memset(raw_d[n][0:P - F2, 1, :], 0.0)
            v.memset(act_a[0:P - F2, 1, :], 0.0)
            for n in range(2):
                for part in range(2):
                    last = v.tensor_copy(aT[n][part][:, :, CAP:2 * P], chunks(zrow[:, 0:3 * (2 * P - CAP)], 2 * P - CAP))
            link(last)
            dve.sem_inc(pads_zero, 1)

            link(v.tensor_tensor(cnt[:, :], run[:, :], base_e[:, :], ALU.subtract))
            v.tensor_copy(cnt_i[:, :], cnt[0:1, :]).then_inc(counted, 1)
            link(v.tensor_tensor(sc[:, 0:OVB, :], spread(cnt[:, :], 1, OVB), spread(thr[:, :], 2, E), ALU.is_gt))
            link(v.tensor_reduce(nblk[:, :], sc[:, 0:OVB, :].rearrange("p a b -> p b a"), AX.X, ALU.add))
            link(v.tensor_tensor(sc[:, :, :], lower[:, :, :], spread(nblk[:, :], 1, E), ALU.mult))
            link(v.tensor_reduce(cum[:, :], sc[:, :, :], AX.X, ALU.add))
            meta_sc, meta_sc2 = sc[0:1, 0:KMAX, :], sc2[0:1, 0:KMAX, :]
            link(v.tensor_tensor(meta_sc, spread(cum[0:1, :], 1, KMAX), spread(ordi[:, :], 2, E), ALU.is_le))
            link(v.tensor_reduce(meta_f[:, 1, :], meta_sc, AX.X, ALU.add))
            link(v.tensor_tensor(meta_sc2, meta_sc, spread(nblk[0:1, :], 1, KMAX), ALU.mult))
            link(v.tensor_reduce(meta_f[:, 2, :], meta_sc2, AX.X, ALU.add))
            link(v.tensor_tensor(meta_f[:, 3, :], ordi[:, :], meta_f[:, 2, :], ALU.subtract))
            link(v.tensor_scalar(meta_f[:, 2, :], meta_f[:, 3, :], float(P), float(CAP), ALU.mult, ALU.add))
            link(v.scalar_tensor_tensor(out=meta_f[:, 3, :], in0=meta_f[:, 1, :], scalar=float(REGION),
                                        in1=meta_f[:, 2, :], op0=ALU.mult, op1=ALU.add))
            link(v.tensor_copy(meta_f[:, 0, :], cum[0:1, E - 1:E].broadcast_to([1, KMAX])))
            link(v.tensor_copy(meta_i[:, :, :], meta_f[:, :, :]))
            link(v.tensor_scalar(meta_half[:, :], meta_i[:, 1, :], 1, None, ALU.logical_shift_right))
            link(v.tensor_copy(meta_i[:, 2, :], meta_half[:, :]))
            dve.sem_inc(meta_ready, 1)
            def plain(ap):
                return ap.bitcast(F32)

            def lo(parts, src, dst_of=lambda t: t[:]):
                return v.tensor_tensor(dst_of(parts[1]), src, plain(dst_of(parts[0])), ALU.subtract)

            def rows_lo(x):
                dve.wait_ge(sg["xhi_done"], x.e + 1 + CREDIT)
                lo(xT[x.par], tpair[:, :, 0:2 * CAP], lambda t: t[:, :, :].rearrange(
                    "p (a c) n -> p a (c n)", a=2)).then_inc(sg["xlo_done"], 1)

            def gu_lo(x):
                dve.wait_ge(sg["whi_done"], x.e + 1 + CREDIT)
                last = lo(gu[x.par], raw_gu[x.par], lambda t: t[:, :, :])
                if x.first_of_pair:
                    last = lo(cgu[x.pair_par], raw_c, lambda t: t[:, :, :, :])
                last.then_inc(sg["wlo_done"], 1)

            def multiply(x):
                dve.wait_ge(sg["alo_done"], x.e + CREDIT)
                dve.wait_ge(sg["silu_done"], (x.e + CREDIT) * 2 + 1)
                v.tensor_tensor(act_a[F2:P, 1, :], act_g[F2:P, 1, :], g_bank[0][F2:P, CAP:2 * CAP],
                                ALU.mult).then_inc(sg["mul_done"], 1)
                dve.wait_ge(sg["gu_done"], (x.e + CREDIT) * 3 + 2)
                v.tensor_tensor(act_a[:, 0, :], act_g[:, 0, :], g_bank[1][:, 0:CAP], ALU.mult).then_inc(
                    sg["mul_done"], 1)
                dve.wait_ge(sg["silu_done"], (x.e + CREDIT) * 2 + 2)
                v.scalar_tensor_tensor(out=act_a[:, 2, :], in0=act_g[:, 2, :], scalar=SMALL_SCALE,
                                       in1=g_bank[2][:, CAP:2 * CAP], op0=ALU.mult, op1=ALU.mult).then_inc(
                                           sg["mul_done"], 1)

            def d_lo(x):
                dve.wait_ge(sg["dhi_done"], x.e + 1 + CREDIT)
                last = lo(dn[x.par], raw_d[x.par], lambda t: t[:, :, :])
                if x.first_of_pair:
                    last = lo(cdn[x.pair_par], raw_cd, lambda t: t[:, :])
                last.then_inc(sg["dlo_done"], 1)

            def a_lo(x):
                dve.wait_ge(sg["ahi_done"], x.e + 1 + CREDIT)
                hi = aT[x.par][0]
                v.tensor_tensor(hi[0:F2, 1, 0:CAP], act_a[F2:P, 1, :], plain(hi[F2:P, 1, 0:CAP]), ALU.subtract)
                lo(aT[x.par], act_a[:, 0:3:2, :], lambda t: t[:, 0:3:2, 0:CAP]).then_inc(sg["alo_done"], 1)

            def y_out(x):
                dve.wait_ge(sg["y1_full"], x.e + 1 + CREDIT)
                dve.wait_ge(added, x.e * (2 * DMA) + (ZEROED - 2 * DMA))
                dve.wait_ge(back_loaded[x.ring], (x.round + 1) * DMA)
                v.tensor_scalar(y_sb[x.par][:, 1, :], y_bank[1][:, :], back[x.ring][:, 1, 1:2].bitcast(F32), None,
                                ALU.mult).then_inc(sg["y1_done"], 1)

            gu_lo(Expert(0, 0))
            rows_lo(Expert(0, 0))

            def step(x):
                if x.ahead(1) is not None:
                    rows_lo(x.ahead(1))
                    gu_lo(x.ahead(1))
                multiply(x)
                d_lo(x)
                a_lo(x)
                if x.ahead(-1) is not None:
                    y_out(x.ahead(-1))

            experts(dve, step)
            y_out(Expert(E // 4 - 1, 3))


            def block_c(k):
                dve.wait_ge(sv["c_xT_full"], k + 1)
                v.tensor_copy(xn1T[:, :, :], chunks(tp[0], P)).then_inc(sv["c_xT_done"], 1)
                dve.wait_ge(sv["c_silu_done"], k + 1)
                v.tensor_tensor(act_a[:, 0, 0:P], act_g[:, 0, 0:P], g_bank[1][:, 0:P], ALU.mult)
                v.tensor_tensor(act_a[F2:P, 1, 0:P], act_g[F2:P, 1, 0:P], g_bank[0][F2:P, P:2 * P], ALU.mult)
                v.scalar_tensor_tensor(out=act_a[:, 2, 0:P], in0=act_g[:, 2, 0:P], scalar=SMALL_SCALE,
                                       in1=g_bank[2][:, P:2 * P], op0=ALU.mult, op1=ALU.mult).then_inc(
                                           sv["c_mul_done"], 1)
                dve.wait_ge(sv["c_y_full"], k + 1)
                dve.wait_ge(sv["c_idx_loaded"], (k + 1) * DMA)
                dve.wait_ge(added, k * DMA + ZEROED + E * 2 * DMA)
                v.tensor_scalar(y_sb[0][:, 0, :], y_bank[0][:, :], idx_c[:, 1:2].bitcast(F32), None,
                                ALU.mult).then_inc(sv["c_y_done"], 1)

            overflow(dve, block_c)

_INS = ['x', 'ctx_2048', 'mask_BxS2_bk0', 'L0_attn_w_q', 'L0_attn_w_k', 'L0_attn_w_v', 'L0_attn_w_o', 'L0_ffn_gate_w',
        'L0_ffn_Wg', 'L0_ffn_Wu', 'L0_ffn_Wd', 'L0_ffn_cWg', 'L0_ffn_cWu', 'L0_ffn_cWd']


def kernel(**inputs):
    import numpy as _np
    import concourse.bacc as _bacc
    from concourse import mybir as _mybir
    from concourse.bass_utils import run_bass_kernel_spmd as _run

    nc = _bacc.Bacc("TRN2", target_bir_lowering=False, num_devices=1)
    arrays, args = {}, []
    for name in _INS:
        a = _np.ascontiguousarray(inputs[name])
        if a.dtype.kind == "b":
            a = a.view(_np.uint32)
        arrays[f"in_{name}_dram"] = a
        args.append(nc.dram_tensor(f"in_{name}_dram", a.shape, _mybir.dt.from_np(a.dtype), kind="ExternalInput").ap())
    shape = inputs['x'].shape
    args.append(nc.dram_tensor("out_0_dram", shape, _mybir.dt.from_np(_np.dtype("float32")), kind="ExternalOutput").ap())
    perceiver_moe(nc, *args)
    r = _run(nc, [arrays], core_ids=[0])
    return r.results[0]["out_0_dram"]
```
